# Optimizing a Trainium2 kernel written in Bass

```python
import numpy as np
import jax
import jax.numpy as jnp

def _softmax(x, axis=-1):
    return jax.nn.softmax(x, axis=axis)

def _gelu(x):
    return jax.nn.gelu(x, approximate=True)

def _silu(x):
    return jax.nn.silu(x)

def _sigmoid(x):
    return jax.nn.sigmoid(x)

def _layernorm(x, axis=-1, eps=1e-05):
    m = jnp.mean(x, axis=axis, keepdims=True)
    v = jnp.var(x, axis=axis, keepdims=True)
    return (x - m) / jnp.sqrt(v + eps)

def _scatter_add(tgt, idx, src, axis=0):
    return tgt.at[idx].add(src)

def _segment_sum(src, seg, n):
    return jax.ops.segment_sum(src, seg, n)
kernel_name = 'mk_adaln_ffn_d1_seqx_r8_abbd2f'

def setup_inputs(seed: int=0):
    np.random.seed(seed)
    _w = jnp.asarray

    def _rec_inputs():
        import jax
        import jax.numpy as jnp
        _rk = jax.random.key(seed)
        x = -0.000125 + 0.9999 * jax.random.normal(jax.random.fold_in(_rk, 1), (4, 256, 256), jnp.float32)
        _lenS = 256 - jax.random.randint(jax.random.fold_in(_rk, 7), (4,), 0, max(1, 256 // 4) + 1, jnp.int32)
        _lenS2 = 256 - jax.random.randint(jax.random.fold_in(_rk, 8), (4,), 0, max(1, 256 // 4) + 1, jnp.int32)
        cond_2048 = 7.82532e-05 + 0.0100527 * jax.random.normal(jax.random.fold_in(_rk, 11), (4, 256), jnp.float32)
        return (x, cond_2048)
    x, cond_2048 = _rec_inputs()

    def _L0_cond_setup():
        import jax, jax.numpy as jnp
        import numpy as np
        NUM_BLOCKS = 8
        NUM_LAYERS = 4
        EPS = 1e-06
        key = jax.random.key(seed)
        ks = jax.random.split(key, 6)
        B, S, H = (4, 512, 256)
        inputs = jax.random.normal(ks[0], (B, S, H), dtype=jnp.float32)
        query_vectors = jax.random.normal(ks[1], (NUM_LAYERS, H), dtype=jnp.float32) * 0.01
        lim = float(np.sqrt(6.0 / (H + H)))
        Wk = jax.random.uniform(ks[2], (H, H), minval=-lim, maxval=lim, dtype=jnp.float32)
        Wo = jax.random.uniform(ks[3], (H, H), minval=-lim, maxval=lim, dtype=jnp.float32)
        rms_weight = jnp.ones((H,), dtype=jnp.float32)
        ln_gamma = jnp.ones((H,), dtype=jnp.float32)
        ln_beta = jnp.zeros((H,), dtype=jnp.float32)
        return {'inputs': inputs, 'layer_idx': 1, 'rms_weight': rms_weight, 'query_vectors': query_vectors, 'Wk': Wk, 'Wo': Wo, 'ln_gamma': ln_gamma, 'ln_beta': ln_beta}
    _L0_cond_all = _L0_cond_setup()
    _L0_cond_in = {k: v for k, v in _L0_cond_all.items() if k in ('rms_weight', 'Wk', 'Wo', 'ln_gamma', 'ln_beta')}
    del _L0_cond_all

    def _L0_ffn_setup():
        import jax, jax.numpy as jnp
        import numpy as np
        K_TOP = 2
        key = jax.random.key(seed)
        k0, k1, k2 = jax.random.split(key, 3)
        B, S, D, E, F = (4, 256, 256, 8, 256)
        x = jax.random.normal(k0, (B, S, D), dtype=jnp.float32)
        Wr = jax.random.normal(k1, (D, E), dtype=jnp.float32) * 0.02
        We = jax.random.normal(k2, (E, D, F), dtype=jnp.float32) * 0.02
        be = jnp.zeros((E, F), dtype=jnp.float32)
        return {'x': x, 'Wr': Wr, 'We': We, 'be': be}
    _L0_ffn_all = _L0_ffn_setup()
    _L0_ffn_in = {k: v for k, v in _L0_ffn_all.items() if k in ('Wr', 'We', 'be')}
    del _L0_ffn_all
    return {'x': x, 'cond_2048': cond_2048, 'L0_cond_rms_weight': _L0_cond_in['rms_weight'], 'L0_cond_Wk': _L0_cond_in['Wk'], 'L0_cond_Wo': _L0_cond_in['Wo'], 'L0_cond_ln_gamma': _L0_cond_in['ln_gamma'], 'L0_cond_ln_beta': _L0_cond_in['ln_beta'], 'L0_ffn_Wr': _L0_ffn_in['Wr'], 'L0_ffn_We': _L0_ffn_in['We'], 'L0_ffn_be': _L0_ffn_in['be']}

def reference(x, cond_2048, L0_cond_rms_weight, L0_cond_Wk, L0_cond_Wo, L0_cond_ln_gamma, L0_cond_ln_beta, L0_ffn_Wr, L0_ffn_We, L0_ffn_be):
    import jax
    import jax.numpy as jnp

    def _L0_cond_ref(inputs, layer_idx, rms_weight, query_vectors, Wk, Wo, ln_gamma, ln_beta):
        import jax, jax.numpy as jnp
        import numpy as np
        NUM_BLOCKS = 8
        NUM_LAYERS = 4
        EPS = 1e-06
        B, S, H = inputs.shape
        block_size = max(1, S // NUM_BLOCKS)
        n_blocks = S // block_size
        block_repr = inputs.reshape(B, n_blocks, block_size, H).sum(axis=2)
        keys = jnp.einsum('bnh,kh->bnk', block_repr, Wk)
        rms = jnp.sqrt(jnp.mean(keys * keys, axis=-1, keepdims=True) + EPS)
        keys = keys / rms * rms_weight
        q = query_vectors[layer_idx]
        scores = jnp.einsum('bnh,h->bn', keys, q)
        attn = jax.nn.softmax(scores, axis=-1)
        attended = jnp.einsum('bn,bnh->bh', attn, block_repr)
        attended = jnp.broadcast_to(attended[:, None, :], (B, S, H))
        proj = jnp.einsum('bsh,kh->bsk', attended, Wo)
        x = inputs + proj
        mu = jnp.mean(x, axis=-1, keepdims=True)
        var = jnp.mean((x - mu) ** 2, axis=-1, keepdims=True)
        out = (x - mu) / jnp.sqrt(var + EPS) * ln_gamma + ln_beta
        return out

    def _L0_ffn_ref(x, Wr, We, be):
        import jax, jax.numpy as jnp
        import numpy as np
        K_TOP = 2
        logits = jnp.einsum('bsd,de->bse', x, Wr)
        w, sel = jax.lax.top_k(logits, K_TOP)
        w = jax.nn.softmax(w, axis=-1)
        E = We.shape[0]
        gate = jnp.einsum('bsk,bske->bse', w, jax.nn.one_hot(sel, E, dtype=w.dtype))
        out = jnp.zeros(x.shape[:2] + (We.shape[2],), dtype=x.dtype)
        for e in range(E):
            out = out + gate[..., e:e + 1] * (jnp.einsum('bsd,df->bsf', x, We[e]) + be[e])
        return out
    x = x + _L0_ffn_ref(_L0_cond_ref(x, 1, L0_cond_rms_weight, cond_2048, L0_cond_Wk, L0_cond_Wo, L0_cond_ln_gamma, L0_cond_ln_beta), L0_ffn_Wr, L0_ffn_We, L0_ffn_be)
    return x

_drawn_inputs = setup_inputs


def setup_inputs(seed=0):
    import zlib

    import numpy as np

    out = dict(_drawn_inputs(seed))
    spreads = {'L0_cond_rms_weight': (1.0, 0.2),
     'L0_cond_ln_gamma': (1.0, 0.2),
     'L0_cond_ln_beta': (0.0, 0.1),
     'L0_ffn_be': (0.0, 0.1)}
    factors = {}
    for name, (base, spread) in spreads.items():
        noise = np.random.default_rng([zlib.crc32(name.encode()), seed]).standard_normal(out[name].shape)
        drawn = base * np.exp(spread * noise) if base else spread * noise
        out[name] = jnp.asarray(drawn.astype(out[name].dtype))
    for name, factor in factors.items():
        out[name] = (out[name] * factor).astype(out[name].dtype)
    return out
```

```python
from contextlib import ExitStack

import concourse.bass as bass
from concourse import mybir

P = 128
F32 = mybir.dt.float32
F32R = mybir.dt.float32r
U32 = mybir.dt.uint32
ALU = mybir.AluOpType
ACT = mybir.ActivationFunctionType
AX_X = mybir.AxisListType.X


def adaln_ffn_kernel(
    nc: bass.Bass,
    x: bass.AP,
    cond: bass.AP,
    rms_weight: bass.AP,
    Wk: bass.AP,
    Wo: bass.AP,
    ln_gamma: bass.AP,
    ln_beta: bass.AP,
    Wr: bass.AP,
    We: bass.AP,
    be: bass.AP,
    out: bass.AP,
):
    B, S, H = x.shape
    E, _, F = We.shape
    N_BLOCKS = 8
    LAYER = 1
    EPS = 1e-6
    T = B * S // P
    C = H // P
    NB = B * N_BLOCKS
    PB = P // NB
    BP = P // B
    BANKS = E * F // 512
    EB = E // BANKS
    PAIRS = T // 2
    assert C == 2 and F == 256 and BANKS == 4 and EB == 2 and T == 8

    x_v = x.rearrange("b s h -> (b s) h").rearrange("(p t) h -> p t h", t=T)
    out_v = out.rearrange("b s h -> (b s) h").rearrange("(p t) h -> p t h", t=T)
    halves = "(c p) -> c p"

    ctx = ExitStack()
    with ctx:
        def sb(name, shape, dt=F32):
            return ctx.enter_context(nc.sbuf_tensor(name, shape, dt))

        def sem(name):
            return ctx.enter_context(nc.semaphore(name))

        x_sb = sb("x_sb", [P, T, H])
        x1 = sb("x1", [P, T, H])
        out_sb = sb("out_sb", [P, T, F])
        wk_sb = sb("wk_sb", [P, C, H])
        wo_sb = sb("wo_sb", [P, C, H])
        wkT = sb("wkT", [P, C, H])
        woT = sb("woT", [P, C, H])
        vec_rows = sb("vec_rows", [4 * C, P])
        vec = sb("vec", [P, 4 * C])
        kq = sb("kq", [P, C])
        u_bc = sb("u_bc", [P, C, P])
        blkT = sb("blkT", [P, C, NB])
        key_sq = sb("key_sq", [P, C, NB])
        k_ln = sb("k_ln", [P, NB])
        k_rstd = sb("k_rstd", [P, NB])
        score = sb("score", [P, NB])
        score_max = sb("score_max", [P, B])
        score_c = sb("score_c", [P, NB])
        prob = sb("prob", [P, NB])
        prob_sum = sb("prob_sum", [P, B])
        prob_rec = sb("prob_rec", [P, B])
        weighted = sb("weighted", [P, C, NB])
        attended = sb("attended", [P, C, B])
        att_bc = sb("att_bc", [P, C, P])
        ident = sb("ident", [P, P])
        ones = sb("ones", [P, P])
        blk_sel = sb("blk_sel", [P, NB])
        iota_e = sb("iota_e", [P, E])
        eps = sb("eps", [P, 1])
        stats = sb("stats", [P, T, 6])
        mv = sb("mv", [P, T, 2])
        var_e = sb("var_e", [P, T])
        v_ln = sb("v_ln", [P, T])
        y0 = sb("y0", [P, T])
        y_a = sb("y_a", [P, T])
        y_b = sb("y_b", [P, T])
        y_c = sb("y_c", [P, T])
        rstd = sb("rstd", [P, T])
        z = sb("z", [P, 2, H])
        h32 = sb("h32", [P, 2, C, P])
        h_hi = sb("h_hi", [P, 2, C, P], F32R)
        h_lo = sb("h_lo", [P, 2, C, P], F32R)
        we_sb = sb("we_sb", [P, E, C, F])
        we_hi = sb("we_hi", [P, E, C, F], F32R)
        we_lo = sb("we_lo", [P, E, C, F], F32R)
        wr_sb = sb("wr_sb", [P, C, E])
        wr_hi = sb("wr_hi", [P, C, E], F32R)
        wr_lo = sb("wr_lo", [P, C, E], F32R)
        be_sb = sb("be_sb", [E, F])
        top_v = sb("top_v", [P, 2, 8])
        top_i = sb("top_i", [P, 2, 8], U32)
        is_1st = sb("is_1st", [P, 2, E])
        is_2nd = sb("is_2nd", [P, 2, E])
        e_2nd = sb("e_2nd", [P, 2, 1])
        e_den = sb("e_den", [P, 2, 1])
        e_rec = sb("e_rec", [P, 2, 1])
        e_both = sb("e_both", [P, 2, E])
        gates = sb("gates", [P, 2, E])
        gatesT = sb("gatesT", [E, 2, P])
        acc = sb("acc", [P, 2, F])
        stage = sb("stage", [P, 2, 5, F])
        part = sb("part", [P, 2, 4, F])

        bank = [ctx.enter_context(nc.psum_tensor(f"bank{n}", [P, 512], F32)) for n in range(8)]
        ring = bank[0:BANKS]
        ps_zT, ps_bias, ps_small = bank[4], bank[5], bank[6]
        ps_proj = bank[7]

        x_in = [sem(f"x_in{i}") for i in range(PAIRS)]
        wk_in, wo_in, vec_in, wr_in, be_in = sem("wk_in"), sem("wo_in"), sem("vec_in"), sem("wr_in"), sem("be_in")
        we_in = [sem(f"we_in{n}") for n in range(BANKS)]
        const_ready = sem("const_ready")
        pool_done, dve_done, act_done = sem("pool_done"), sem("dve_done"), sem("act_done")
        vecT_ready, vec_ready = sem("vecT_ready"), sem("vec_ready")
        wkT_raw, wkT_ready = sem("wkT_raw"), sem("wkT_ready")
        woT_raw, woT_ready = sem("woT_raw"), sem("woT_ready")
        kq_ready, u_raw, u_ready = sem("kq_ready"), sem("u_raw"), sem("u_ready")
        blk_raw, blk0_ready, blk1_ready = sem("blk_raw"), sem("blk0_ready"), sem("blk1_ready")
        keys_ready, dots_ready, key_sq_ready, key_ss_ready = (
            sem("keys_ready"), sem("dots_ready"), sem("key_sq_ready"), sem("key_ss_ready"))
        k_rstd_ready, score_ready, prob_ready = sem("k_rstd_ready"), sem("score_ready"), sem("prob_ready")
        att_ready, proj_ready = sem("att_ready"), sem("proj_ready")
        var_ready, y0_ready = sem("var_ready"), sem("y0_ready")
        wr_ready, we_hi_ready, we_lo_ready = sem("wr_ready"), sem("we_hi_ready"), sem("we_lo_ready")
        z_ready, zT_ready, h_ready = sem("z_ready"), sem("zT_ready"), sem("h_ready")
        hi_ready, lo_ready = sem("hi_ready"), sem("lo_ready")
        logits_ready, top_ready, e_ready, gates_ready = (
            sem("logits_ready"), sem("top_ready"), sem("e_ready"), sem("gates_ready"))
        gatesT_raw, gatesT_ready = sem("gatesT_raw"), sem("gatesT_ready")
        bias_ready, bias_staged = sem("bias_ready"), sem("bias_staged")
        bank_ready = [sem(f"bank_ready{n}") for n in range(BANKS)]
        bank_free = [sem(f"bank_free{n}") for n in range(BANKS)]
        out_ready, stored = sem("out_ready"), sem("stored")

        block = ctx.enter_context(nc.Block())

        def half(vector, row):
            return vec_rows[C * row:C * (row + 1), :], vector.rearrange(halves, p=P)

        @block.sync
        def _(sp):
            for i in range(PAIRS):
                sp.dma_start(x_sb[:, 2 * i:2 * i + 2, :], x_v[:, 2 * i:2 * i + 2, :]).then_inc(x_in[i], 16)
            sp.dma_start(wo_sb[:], Wo.rearrange("(c p) h -> p c h", p=P)).then_inc(wo_in, 16)
            for n in range(BANKS):
                for e in range(EB * n, EB * (n + 1)):
                    sp.dma_start(we_sb[:, e], We[e].rearrange("(c p) f -> p c f", p=P)).then_inc(we_in[n], 16)
            with sp.Fori(0, PAIRS) as i:
                sp.wait_ge(out_ready, 2 * i + 2)
                sp.dma_start(out_v[:, bass.ds(2 * i, 2), :], out_sb[:, bass.ds(2 * i, 2), :]).then_inc(stored, 16)
            sp.wait_ge(stored, 16 * PAIRS)

        @block.gpsimd
        def _(pool):
            nc.gpsimd.memset(ones[:], 1.0).then_inc(pool_done, 1)
            nc.gpsimd.memset(eps[:], EPS)
            nc.gpsimd.iota(iota_e[:], pattern=[[1, E]], base=0, channel_multiplier=0,
                           allow_small_or_imprecise_dtypes=True)
            pool.wait_ge(pool_done, 1)
            nc.gpsimd.affine_select(out=ident[:], in_=ones[:], compare_op=ALU.is_equal, fill=0.0, base=0,
                                    pattern=[[-1, P]], channel_multiplier=1)
            nc.gpsimd.affine_select(out=blk_sel[:], in_=ones[:, 0:NB], compare_op=ALU.is_ge, fill=0.0, base=0,
                                    pattern=[[-PB, NB]], channel_multiplier=1).then_inc(pool_done, 1)
            pool.wait_ge(pool_done, 2)
            nc.gpsimd.affine_select(out=blk_sel[:], in_=blk_sel[:], compare_op=ALU.is_ge, fill=0.0, base=PB - 1,
                                    pattern=[[PB, NB]], channel_multiplier=-1).then_inc(const_ready, 1)
            for n in range(BANKS):
                pool.wait_ge(we_hi_ready, n + 1)
                es = slice(EB * n, EB * (n + 1))
                nc.gpsimd.tensor_sub(we_lo[:, es], we_sb[:, es], we_hi[:, es].bitcast(F32)).then_inc(we_lo_ready, 1)

            def sum_up(t, s, done):
                pool.wait_ge(bank_free[1], t + 1)
                nc.gpsimd.tensor_add(part[:, s, 0], stage[:, s, 0], stage[:, s, 1]).then_inc(pool_done, 1)
                pool.wait_ge(bias_staged, t + 1)
                pool.wait_ge(pool_done, done + 1)
                nc.gpsimd.tensor_add(part[:, s, 1], stage[:, s, 2], part[:, s, 0]).then_inc(pool_done, 1)
                pool.wait_ge(bank_free[2], t + 1)
                pool.wait_ge(pool_done, done + 2)
                nc.gpsimd.tensor_add(part[:, s, 2], acc[:, s], part[:, s, 1]).then_inc(pool_done, 1)
                pool.wait_ge(bank_free[3], t + 1)
                pool.wait_ge(pool_done, done + 3)
                nc.gpsimd.tensor_add(part[:, s, 3], stage[:, s, 3], part[:, s, 2]).then_inc(pool_done, 1)
                pool.wait_ge(pool_done, done + 4)
                nc.gpsimd.tensor_add(out_sb[:, t, :], stage[:, s, 4], part[:, s, 3]).then_inc(out_ready, 1)

            SUMS = 4
            with pool.Fori(0, PAIRS) as i:
                sum_up(2 * i, 0, 2 + SUMS * (2 * i))
                sum_up(2 * i + 1, 1, 2 + SUMS * (2 * i + 1))

        @block.scalar
        def _(act):
            act.dma_start(wk_sb[:], Wk.rearrange("(c p) h -> p c h", p=P)).then_inc(wk_in, 16)
            for row, vector in enumerate((ln_gamma, ln_beta, rms_weight, cond[LAYER])):
                act.dma_start(*half(vector, row)).then_inc(vec_in, 16)
            act.dma_start(wr_sb[:], Wr.rearrange("(c p) e -> p c e", p=P)).then_inc(wr_in, 16)
            act.dma_start(be_sb[:], be).then_inc(be_in, 16)
            nc.scalar.preload_act_table_set("natural_log_exp_and_others")
            act.wait_ge(wkT_raw, 1)
            nc.scalar.activation(wkT[:].rearrange("p c h -> p (c h)"), bank[0][:], ACT.Identity).then_inc(wkT_ready, 1)
            act.wait_ge(blk_raw, 1)
            nc.scalar.activation(blkT[:, 1], bank[4][:, 0:NB], ACT.Identity).then_inc(blk1_ready, 1)
            act.wait_ge(keys_ready, 1)
            nc.scalar.activation(key_sq[:], bank[5][:, 0:C * NB].rearrange("p (c n) -> p c n", c=C),
                                 ACT.Square).then_inc(key_sq_ready, 1)
            act.wait_ge(key_ss_ready, 1)
            nc.scalar.activation(k_ln[:], bank[7][:, 0:NB], ACT.Ln, bias=eps[:], scale=1.0 / H).then_inc(act_done, 1)
            act.wait_ge(act_done, 1)
            nc.scalar.activation(k_rstd[:], k_ln[:], ACT.Exp, scale=-0.5).then_inc(k_rstd_ready, 1)
            act.wait_ge(woT_raw, 1)
            nc.scalar.activation(woT[:].rearrange("p c h -> p (c h)"), bank[1][:], ACT.Identity).then_inc(woT_ready, 1)
            act.wait_ge(score_ready, 1)
            nc.scalar.activation(prob[:], score_c[:], ACT.Exp).then_inc(prob_ready, 1)

            def high_weights(n):
                act.wait_ge(we_in[n], 16 * EB)
                es = slice(EB * n, EB * (n + 1))
                nc.scalar.copy(we_hi[:, es], we_sb[:, es]).then_inc(we_hi_ready, 1)

            high_weights(0)
            high_weights(1)

            def rstd_start(k, done, t0, t1):
                act.wait_ge(var_ready, k)
                nc.scalar.activation(v_ln[:, t0:t1], mv[:, t0:t1, 1], ACT.Ln, bias=eps[:]).then_inc(act_done, 1)
                act.wait_ge(act_done, done)
                nc.scalar.activation(y0[:, t0:t1], v_ln[:, t0:t1], ACT.Exp, scale=-0.5).then_inc(y0_ready, 1)

            def scale_shift(u, s):
                act.wait_ge(zT_ready, u + 1)
                if not isinstance(u, int) or u >= 2:
                    act.wait_ge(lo_ready, u - 1)
                for c in range(C):
                    last = nc.scalar.activation(h32[:, s, c], ps_zT[:, c * P:(c + 1) * P], ACT.Identity,
                                                bias=vec[:, C + c:C + c + 1], scale=vec[:, c:c + 1])
                last.then_inc(h_ready, 1)

            def second_gate(u, s):
                act.wait_ge(top_ready, u + 1)
                nc.scalar.activation(e_2nd[:, s], top_v[:, s, 0:1], ACT.Exp, bias=top_v[:, s, 1:2],
                                     scale=-1.0).then_inc(e_ready, 1)

            def copy_gatesT(t, s):
                act.wait_ge(gatesT_raw, t + 1)
                nc.scalar.activation(gatesT[:, s], ps_small[0:E, 128:128 + P], ACT.Identity).then_inc(gatesT_ready, 1)

            def gated(t, s, n, k):
                act.wait_ge(bank_ready[n], t + 1)
                for j in range(EB):
                    e = EB * n + j
                    last = nc.scalar.activation(stage[:, s, k + j], ring[n][:, j * F:(j + 1) * F], ACT.Copy,
                                                scale=gates[:, s, e:e + 1])
                last.then_inc(bank_free[n], 1)

            def stage_bias(t, s):
                act.wait_ge(bias_ready, t + 1)
                nc.scalar.activation(stage[:, s, 2], ps_bias[:, 0:F], ACT.Identity).then_inc(bias_staged, 1)

            rstd_start(1, 2, 0, 2)
            act.wait_ge(vec_ready, 1)
            scale_shift(0, 0)
            high_weights(2)
            high_weights(3)
            second_gate(0, 0)
            rstd_start(2, 3, 2, T)

            def step(t, s, last):
                copy_gatesT(t, s)
                if not last:
                    scale_shift(t + 1, 1 - s)
                if not isinstance(t, int) or t >= 2:
                    act.wait_ge(out_ready, t - 1)
                gated(t, s, 1, 0)
                stage_bias(t, s)
                if not last:
                    second_gate(t + 1, 1 - s)
                gated(t, s, 3, 3)

            step(0, 0, False)
            step(1, 1, False)
            with act.Fori(1, PAIRS - 1) as i:
                step(2 * i, 0, False)
                step(2 * i + 1, 1, False)
            step(T - 2, 0, False)
            step(T - 1, 1, True)

        @block.vector
        def _(dve):
            links = [0]

            def link(ins):
                links[0] += 1
                ins.then_inc(dve_done, 1)
                dve.wait_ge(dve_done, links[0])

            dve.wait_ge(vecT_ready, 1)
            nc.vector.tensor_copy(vec[:], bank[2][:, 0:4 * C]).then_inc(vec_ready, 1)
            dve.wait_ge(vec_ready, 1)
            nc.vector.tensor_tensor(kq[:], vec[:, 2 * C:3 * C], vec[:, 3 * C:4 * C], ALU.mult).then_inc(kq_ready, 1)
            dve.wait_ge(u_raw, 1)
            for c in range(C):
                last = nc.vector.tensor_scalar(u_bc[:, c], ones[:], bank[3][:, c:c + 1], None, ALU.mult)
            last.then_inc(u_ready, 1)
            dve.wait_ge(wr_in, 16)
            link(nc.vector.tensor_copy(wr_hi[:], wr_sb[:]))
            nc.vector.tensor_sub(wr_lo[:], wr_sb[:], wr_hi[:].bitcast(F32)).then_inc(wr_ready, 1)
            dve.wait_ge(blk_raw, 1)
            nc.vector.tensor_copy(blkT[:, 0], bank[3][:, 0:NB]).then_inc(blk0_ready, 1)
            dve.wait_ge(k_rstd_ready, 1)
            link(nc.vector.tensor_tensor(score[:], bank[6][:, 0:NB], k_rstd[:], ALU.mult))
            by_seq = "p (b n) -> p b n"
            link(nc.vector.tensor_reduce(score_max[:], score[:].rearrange(by_seq, b=B), AX_X, ALU.max))
            nc.vector.tensor_tensor(score_c[:].rearrange(by_seq, b=B), score[:].rearrange(by_seq, b=B),
                                    score_max[:].unsqueeze(2).to_broadcast([P, B, N_BLOCKS]),
                                    ALU.subtract).then_inc(score_ready, 1)
            dve.wait_ge(prob_ready, 1)
            nc.vector.tensor_reduce(prob_sum[:], prob[:].rearrange(by_seq, b=B), AX_X, ALU.add).then_inc(dve_done, 1)
            link(nc.vector.tensor_tensor(weighted[:], blkT[:], prob[:].unsqueeze(1).to_broadcast([P, C, NB]),
                                         ALU.mult))
            links[0] += 1
            dve.wait_ge(dve_done, links[0])
            nc.vector.reciprocal(prob_rec[:], prob_sum[:]).then_inc(dve_done, 1)
            links[0] += 1
            link(nc.vector.tensor_reduce(attended[:], weighted[:].rearrange("p c (b n) -> p c b n", b=B), AX_X, ALU.add))
            nc.vector.tensor_tensor(att_bc[:].rearrange("p c (b r) -> p c b r", b=B),
                                    attended[:].unsqueeze(3).to_broadcast([P, C, B, BP]),
                                    prob_rec[:].unsqueeze(1).unsqueeze(3).to_broadcast([P, C, B, BP]),
                                    ALU.mult).then_inc(att_ready, 1)

            def tile_stats(i):
                ts = slice(2 * i, 2 * i + 2)
                link(nc.vector.tensor_tensor(x1[:, ts, :], x_sb[:, ts, :],
                                             ps_proj[:, 0:H].unsqueeze(1).to_broadcast([P, 2, H]), ALU.add))
                for t in (2 * i, 2 * i + 1):
                    last = nc.vector.bn_stats(stats[:, t], x1[:, t])
                link(last)
                for t in (2 * i, 2 * i + 1):
                    last = nc.vector.bn_aggr(mv[:, t], stats[:, t])
                return last

            def refine(k, t0, t1):
                ts = slice(t0, t1)
                link(nc.vector.tensor_scalar(var_e[:, ts], mv[:, ts, 1], EPS, None, ALU.add))
                dve.wait_ge(y0_ready, k)
                link(nc.vector.tensor_tensor(y_a[:, ts], y0[:, ts], y0[:, ts], ALU.mult))
                link(nc.vector.tensor_tensor(y_b[:, ts], y_a[:, ts], var_e[:, ts], ALU.mult))
                link(nc.vector.tensor_scalar(y_c[:, ts], y_b[:, ts], -0.5, 1.5, ALU.mult, ALU.add))
                link(nc.vector.tensor_tensor(rstd[:, ts], y0[:, ts], y_c[:, ts], ALU.mult))

            def normalise(u, s):
                if not isinstance(u, int) or u >= 2:
                    dve.wait_ge(zT_ready, u - 1)
                nc.vector.tensor_scalar(z[:, s], x1[:, u], mv[:, u, 0:1], rstd[:, bass.ds(u, 1)],
                                        ALU.subtract, ALU.mult).then_inc(z_ready, 1)

            def split(u, s):
                dve.wait_ge(h_ready, u + 1)
                if not isinstance(u, int) or u >= 2:
                    dve.wait_ge(bank_ready[BANKS - 1], u - 1)
                nc.vector.tensor_copy(h_hi[:, s], h32[:, s]).then_inc(hi_ready, 1)
                dve.wait_ge(hi_ready, u + 1)
                nc.vector.tensor_sub(h_lo[:, s], h32[:, s], h_hi[:, s].bitcast(F32)).then_inc(lo_ready, 1)

            def top_two(u, s, done):
                dve.wait_ge(const_ready, 1)
                dve.wait_ge(logits_ready, u + 1)
                nc.vector.max(top_v[:, s], ps_small[:, 0:E]).then_inc(top_ready, 1)
                dve.wait_ge(const_ready, 1)
                dve.wait_ge(top_ready, u + 1)
                nc.vector.max_index(top_i[:, s], top_v[:, s], ps_small[:, 0:E]).then_inc(dve_done, 1)
                dve.wait_ge(dve_done, done + 1)
                nc.vector.tensor_scalar(is_1st[:, s], iota_e[:], top_i[:, s, 0:1], None, ALU.is_equal)
                nc.vector.tensor_scalar(is_2nd[:, s], iota_e[:], top_i[:, s, 1:2], None,
                                        ALU.is_equal).then_inc(dve_done, 1)

            def gate(u, s, done):
                dve.wait_ge(e_ready, u + 1)
                dve.wait_ge(dve_done, done + 2)
                nc.vector.tensor_scalar(e_den[:, s], e_2nd[:, s], 1.0, None, ALU.add).then_inc(dve_done, 1)
                nc.vector.scalar_tensor_tensor(out=e_both[:, s], in0=is_2nd[:, s], scalar=e_2nd[:, s], in1=is_1st[:, s],
                                               op0=ALU.mult, op1=ALU.add)
                dve.wait_ge(dve_done, done + 3)
                nc.vector.reciprocal(e_rec[:, s], e_den[:, s]).then_inc(dve_done, 1)
                dve.wait_ge(dve_done, done + 4)
                nc.vector.tensor_scalar(gates[:, s], e_both[:, s], e_rec[:, s], None, ALU.mult).then_inc(gates_ready, 1)

            def add_gated(t, s, n, done):
                dve.wait_ge(bank_ready[n], t + 1)
                for j in range(EB):
                    e = EB * n + j
                    before = x_sb[:, t] if e == 0 else acc[:, s]
                    ins = nc.vector.scalar_tensor_tensor(out=acc[:, s], in0=ring[n][:, j * F:(j + 1) * F],
                                                         scalar=gates[:, s, e:e + 1], in1=before,
                                                         op0=ALU.mult, op1=ALU.add)
                    if j < EB - 1:
                        ins.then_inc(dve_done, 1)
                        dve.wait_ge(dve_done, done + 1)
                    else:
                        ins.then_inc(bank_free[n], 1)

            PREP = 4
            SUMS = 2

            dve.wait_ge(proj_ready, 1)
            tile_stats(0).then_inc(var_ready, 1)
            dve.wait_ge(var_ready, 1)
            refine(1, 0, 2)
            normalise(0, 0)
            for i in range(1, PAIRS):
                last = tile_stats(i)
                if i < PAIRS - 1:
                    link(last)
                if i == 1:
                    split(0, 0)
            last.then_inc(var_ready, 1)
            base = links[0]
            top_two(0, 0, base)
            gate(0, 0, base)
            links[0] += PREP
            dve.wait_ge(var_ready, 2)
            refine(2, 2, T)
            base = links[0]

            def step(t, s, done, last):
                if not last:
                    normalise(t + 1, 1 - s)
                dve.wait_ge(gates_ready, t + 1)
                if not isinstance(t, int) or t >= 2:
                    dve.wait_ge(out_ready, t - 1)
                add_gated(t, s, 0, done)
                if not last:
                    split(t + 1, 1 - s)
                dve.wait_ge(bank_free[0], t + 1)
                add_gated(t, s, 2, done + 1)
                if not last:
                    top_two(t + 1, 1 - s, done + 2)
                    gate(t + 1, 1 - s, done + 2)

            STEP = SUMS + PREP
            step(0, 0, base, False)
            step(1, 1, base + STEP, False)
            with dve.Fori(1, PAIRS - 1) as i:
                step(2 * i, 0, base + STEP * (2 * i), False)
                step(2 * i + 1, 1, base + STEP * (2 * i + 1), False)
            step(T - 2, 0, base + STEP * (T - 2), False)
            step(T - 1, 1, base + STEP * (T - 1), True)

        @block.tensor
        def _(pe):
            pe.wait_ge(const_ready, 1)
            pe.wait_ge(vec_in, 16 * 4)
            nc.tensor.transpose(bank[2][:, 0:4 * C], vec_rows[:], ident[0:4 * C, 0:4 * C]).then_inc(vecT_ready, 1)

            def transpose_weights(dst, w):
                for c in range(C):
                    for k in range(C):
                        last = nc.tensor.transpose(dst[:, c * H + k * P:c * H + (k + 1) * P],
                                                   w[:, k, c * P:(c + 1) * P], ident[:])
                return last

            pe.wait_ge(wk_in, 16)
            transpose_weights(bank[0], wk_sb).then_inc(wkT_raw, 1)
            pe.wait_ge(kq_ready, 1)
            for c in range(C):
                for k in range(C):
                    last = nc.tensor.matmul(bank[3][:, c:c + 1], wk_sb[:, k, c * P:(c + 1) * P], kq[:, k:k + 1],
                                            start=(k == 0), stop=(k == C - 1))
            last.then_inc(u_raw, 1)
            pe.wait_ge(u_ready, 1)
            for t in range(T):
                if t % 2 == 0:
                    pe.wait_ge(x_in[t // 2], 16)
                for c in range(C):
                    last = nc.tensor.matmul(bank[3 + c][:, 0:NB], x_sb[:, t, c * P:(c + 1) * P], blk_sel[:],
                                            start=(t == 0), stop=(t == T - 1))
            last.then_inc(blk_raw, 1)
            pe.wait_ge(blk0_ready, 1)
            pe.wait_ge(blk1_ready, 1)
            pe.wait_ge(wkT_ready, 1)
            for k in range(C):
                for c in range(C):
                    last = nc.tensor.matmul(bank[5][:, k * NB:(k + 1) * NB], wkT[:, c, k * P:(k + 1) * P], blkT[:, c],
                                            start=(c == 0), stop=(c == C - 1))
            last.then_inc(keys_ready, 1)
            for c in range(C):
                last = nc.tensor.matmul(bank[6][:, 0:NB], u_bc[:, c], blkT[:, c], start=(c == 0), stop=(c == C - 1))
            last.then_inc(dots_ready, 1)
            pe.wait_ge(key_sq_ready, 1)
            for c in range(C):
                last = nc.tensor.matmul(bank[7][:, 0:NB], ones[:], key_sq[:, c], start=(c == 0), stop=(c == C - 1))
            last.then_inc(key_ss_ready, 1)
            pe.wait_ge(wo_in, 16)
            transpose_weights(bank[1], wo_sb).then_inc(woT_raw, 1)
            pe.wait_ge(woT_ready, 1)
            pe.wait_ge(att_ready, 1)
            for c in range(C):
                last = nc.tensor.matmul(ps_proj[:, 0:H], att_bc[:, c], woT[:, c], start=(c == 0), stop=(c == C - 1))
            last.then_inc(proj_ready, 1)

            def transpose_tile(u, s):
                pe.wait_ge(z_ready, u + 1)
                for c in range(C):
                    last = nc.tensor.transpose(ps_zT[:, c * P:(c + 1) * P], z[:, s, c * P:(c + 1) * P], ident[:])
                last.then_inc(zT_ready, 1)

            def route(u, s):
                pe.wait_ge(lo_ready, u + 1)
                terms = [(h, w, c) for c in range(C) for h, w in
                         ((h_hi, wr_hi), (h_hi, wr_lo), (h_lo, wr_hi), (h_lo, wr_lo))]
                for k, (h, w, c) in enumerate(terms):
                    last = nc.tensor.matmul(ps_small[:, 0:E], h[:, s, c], w[:, c],
                                            start=(k == 0), stop=(k == len(terms) - 1))
                last.then_inc(logits_ready, 1)

            def experts(t, s, n):
                if not isinstance(t, int) or t >= 1:
                    pe.wait_ge(bank_free[n], t)
                if isinstance(t, int) and t == 0:
                    pe.wait_ge(we_lo_ready, n + 1)
                terms = [(h, w, c) for c in range(C) for h, w in ((h_hi, we_hi), (h_hi, we_lo), (h_lo, we_hi))]
                for k, (h, w, c) in enumerate(terms):
                    last = nc.tensor.matmul(ring[n][:], h[:, s, c], w[:, EB * n:EB * (n + 1), c],
                                            start=(k == 0), stop=(k == len(terms) - 1))
                last.then_inc(bank_ready[n], 1)

            def transpose_gates(t, s):
                pe.wait_ge(gates_ready, t + 1)
                nc.tensor.transpose(ps_small[0:E, 128:128 + P], gates[:, s], ident[:]).then_inc(gatesT_raw, 1)

            def bias(t, s):
                pe.wait_ge(gatesT_ready, t + 1)
                if not isinstance(t, int) or t >= 1:
                    pe.wait_ge(bias_staged, t)
                nc.tensor.matmul(ps_bias[:, 0:F], gatesT[:, s], be_sb[:], start=True, stop=True).then_inc(bias_ready, 1)

            def step(t, s, last):
                experts(t, s, 0)
                transpose_gates(t, s)
                if not last:
                    transpose_tile(t + 1, 1 - s)
                experts(t, s, 1)
                bias(t, s)
                experts(t, s, 2)
                if not last:
                    route(t + 1, 1 - s)
                experts(t, s, 3)

            transpose_tile(0, 0)
            pe.wait_ge(wr_ready, 1)
            route(0, 0)
            pe.wait_ge(be_in, 16)
            step(0, 0, False)
            step(1, 1, False)
            with pe.Fori(1, PAIRS - 1) as i:
                step(2 * i, 0, False)
                step(2 * i + 1, 1, False)
            step(T - 2, 0, False)
            step(T - 1, 1, True)


_INS = ['x', 'cond_2048', 'L0_cond_rms_weight', 'L0_cond_Wk', 'L0_cond_Wo', 'L0_cond_ln_gamma', 'L0_cond_ln_beta',
        'L0_ffn_Wr', 'L0_ffn_We', 'L0_ffn_be']
_OUTS = [((4, 256, 256), 'float32')]


def kernel(**inputs):
    import numpy as _np
    import concourse.bacc as _bacc
    from concourse import mybir as _mybir
    from concourse.bass_utils import run_bass_kernel_spmd as _run

    nc = _bacc.Bacc("TRN2", target_bir_lowering=False, num_devices=1)
    arrays, args = {}, []
    for name in _INS:
        a = _np.ascontiguousarray(inputs[name])
        arrays[f"in_{name}_dram"] = a
        args.append(nc.dram_tensor(f"in_{name}_dram", a.shape, _mybir.dt.from_np(a.dtype), kind="ExternalInput").ap())
    for i, (shape, dtype) in enumerate(_OUTS):
        dt = _mybir.dt.from_np(_np.dtype(dtype))
        args.append(nc.dram_tensor(f"out_{i}_dram", shape, dt, kind="ExternalOutput").ap())
    adaln_ffn_kernel(nc, *args)
    r = _run(nc, [arrays], core_ids=[0])
    got = tuple(r.results[0][f"out_{i}_dram"] for i in range(len(_OUTS)))
    return got[0]
```

```python
from contextlib import ExitStack

import concourse.bass as bass
from concourse import mybir

P = 128
F32 = mybir.dt.float32
F32R = mybir.dt.float32r
BF16 = mybir.dt.bfloat16
U32 = mybir.dt.uint32
ALU = mybir.AluOpType
ACT = mybir.ActivationFunctionType
AX_X = mybir.AxisListType.X


class Counted:

    def __init__(self, engine, semaphore):
        self.engine, self.semaphore, self.value = engine, semaphore, 0

    def mark(self, instruction):
        instruction.then_inc(self.semaphore, 1)
        self.value = self.value + 1
        return self.value

    def link(self, instruction):
        self.engine.wait_ge(self.semaphore, self.mark(instruction))


def adaln_ffn_kernel(
    nc: bass.Bass,
    x: bass.AP,
    cond: bass.AP,
    rms_weight: bass.AP,
    Wk: bass.AP,
    Wo: bass.AP,
    ln_gamma: bass.AP,
    ln_beta: bass.AP,
    Wr: bass.AP,
    We: bass.AP,
    be: bass.AP,
    out: bass.AP,
):
    B, S, H = x.shape
    E, _, F = We.shape
    N_BLOCKS = 8
    LAYER = 1
    EPS = 1e-6
    T = B * S // P
    C = H // P
    NB = B * N_BLOCKS
    PB = P // NB
    BP = P // B
    BANKS = E * F // 512
    EB = E // BANKS
    PAIRS = T // 2
    LO_DVE = (0, 4)
    WARM = (6, 10, 6, 3, 1)
    Q = 32
    assert C == 2 and F == 256 and BANKS == 4 and EB == 2 and T == 8

    x_v = x.rearrange("b s h -> (b s) h").rearrange("(p t) h -> p t h", t=T)
    out_v = out.rearrange("b s h -> (b s) h").rearrange("(p t) h -> p t h", t=T)
    halves = "(c p) -> c p"

    ctx = ExitStack()
    with ctx:
        def sb(name, shape, dt=F32):
            return ctx.enter_context(nc.sbuf_tensor(name, shape, dt))

        def sem(name):
            return ctx.enter_context(nc.semaphore(name))

        x_sb = sb("x_sb", [P, T, H])
        x1 = sb("x1", [P, T, H])
        out_sb = sb("out_sb", [P, T, F])
        wk_sb = sb("wk_sb", [P, C, H])
        wo_sb = sb("wo_sb", [P, C, H])
        wkT = sb("wkT", [P, C, H])
        woT = sb("woT", [P, C, H])
        vec_rows = sb("vec_rows", [4 * C, P])
        vec = sb("vec", [P, 4 * C])
        kq = sb("kq", [P, C])
        u_sb = sb("u_sb", [P, C])
        x_pair = sb("x_pair", [P, 2, 2, H])
        x_sum = sb("x_sum", [P, H])
        blkT = sb("blkT", [P, C, NB])
        to_sum = sb("to_sum", [P, C, 2, NB])
        proj_sb = sb("proj_sb", [P, H])
        k_ln = sb("k_ln", [P, NB])
        k_rstd = sb("k_rstd", [P, NB])
        score = sb("score", [P, NB])
        score_max = sb("score_max", [P, B])
        score_c = sb("score_c", [P, NB])
        prob = sb("prob", [P, NB])
        prob_sum = sb("prob_sum", [P, B])
        prob_rec = sb("prob_rec", [P, B])
        weighted = sb("weighted", [P, C, NB])
        attended = sb("attended", [P, C, B])
        att_bc = sb("att_bc", [P, C, P])
        ident = sb("ident", [P, P])
        ones = sb("ones", [P, P])
        blk_sel = sb("blk_sel", [P, NB])
        iota_e = sb("iota_e", [P, E])
        eps = sb("eps", [P, 1])
        stats = sb("stats", [P, T, 6])
        mv = sb("mv", [P, T, 2])
        v_ln = sb("v_ln", [P, T])
        y0 = sb("y0", [P, T])
        y_a = sb("y_a", [P, T])
        y_b = sb("y_b", [P, T])
        y_c = sb("y_c", [P, T])
        rstd = sb("rstd", [P, T])
        z = sb("z", [P, 2, H])
        h32 = sb("h32", [P, 2, C, P])
        h_hi = sb("h_hi", [P, 2, C, P], F32R)
        h_lo = sb("h_lo", [P, 2, C, P], F32R)
        we_sb = sb("we_sb", [P, E, C, F])
        we_hi = sb("we_hi", [P, E, C, F], F32R)
        we_lo = sb("we_lo", [P, E, C, F], F32R)
        wr_sb = sb("wr_sb", [P, C, E])
        wr_2 = sb("wr_2", [P, C, 2, E], F32R)
        be_sb = sb("be_sb", [3 * Q, F])
        be_3 = sb("be_3", [3 * Q, F], F32R)
        logits = sb("logits", [P, 2, E])
        warm = sb("warm", [P, 512], BF16)
        top_v = sb("top_v", [P, 2, 8])
        top_i = sb("top_i", [P, 2, 8], U32)
        is_1st = sb("is_1st", [P, 2, E])
        is_2nd = sb("is_2nd", [P, 2, E])
        e_2nd = sb("e_2nd", [P, 2, 1])
        e_den = sb("e_den", [P, 2, 1])
        e_rec = sb("e_rec", [P, 2, 1])
        e_both = sb("e_both", [P, 2, E])
        gates = sb("gates", [P, 2, E])
        gates_3 = sb("gates_3", [P, 2, 3 * Q])
        gatesT = sb("gatesT", [3 * Q, 2, P], F32R)
        acc = sb("acc", [P, 2, F])
        stage = sb("stage", [P, 2, 5, F])
        part = sb("part", [P, 2, 4, F])

        bank = [ctx.enter_context(nc.psum_tensor(f"bank{n}", [P, 512], F32)) for n in range(8)]
        ring = bank[0:BANKS]
        ps_zT, ps_bias, ps_small, ps_proj = bank[4], bank[5], bank[6], bank[7]
        LOGITS, GATES_T = slice(0, 2 * E), slice(P, 2 * P)

        x_in = [sem(f"x_in{i}") for i in range(PAIRS)]
        wk_in, wo_in, vec_in, wr_in, be_in = (sem("wk_in"), sem("wo_in"), sem("vec_in"), sem("wr_in"),
                                             sem("be_in"))
        affine_in = sem("affine_in")
        we_in = [sem(f"we_in{e}") for e in range(E)]
        const_ready = sem("const_ready")
        pool_done, dve_done, act_done = sem("pool_done"), sem("dve_done"), sem("act_done")
        vecT_ready, vec_ready = sem("vecT_ready"), sem("vec_ready")
        wkT_raw, wkT_ready = sem("wkT_raw"), sem("wkT_ready")
        woT_raw, woT_ready = sem("woT_raw"), sem("woT_ready")
        kq_ready, u_raw, u_ready = sem("kq_ready"), sem("u_raw"), sem("u_ready")
        x_sum_ready, blk_raw, blk_ready = sem("x_sum_ready"), sem("blk_raw"), sem("blk_ready")
        keys_ready, key_sq_ready, ub_ready, key_sums_ready = (
            sem("keys_ready"), sem("key_sq_ready"), sem("ub_ready"), sem("key_sums_ready"))
        x1_0_ready, proj_copied, x1_ready = sem("x1_0_ready"), sem("proj_copied"), sem("x1_ready")
        h0_ready, zeros_ready, be_ready = sem("h0_ready"), sem("zeros_ready"), sem("be_ready")
        warm_ready, logits_summed = sem("warm_ready"), sem("logits_summed")
        k_rstd_ready, score_ready, prob_ready = sem("k_rstd_ready"), sem("score_ready"), sem("prob_ready")
        att_ready, proj_ready = sem("att_ready"), sem("proj_ready")
        var_ready, y0_ready = sem("var_ready"), sem("y0_ready")
        wr_ready, we_hi_ready, we_lo_ready, we_lo_dve = (
            sem("wr_ready"), sem("we_hi_ready"), sem("we_lo_ready"), sem("we_lo_dve"))
        z_ready, zT_ready, h_ready = sem("z_ready"), sem("zT_ready"), sem("h_ready")
        hi_ready, lo_ready = sem("hi_ready"), sem("lo_ready")
        logits_ready, top_ready, e_ready, gates_ready = (
            sem("logits_ready"), sem("top_ready"), sem("e_ready"), sem("gates_ready"))
        parts_ready = sem("parts_ready")
        gatesT_raw, gatesT_ready = sem("gatesT_raw"), sem("gatesT_ready")
        bias_ready, bias_staged = sem("bias_ready"), sem("bias_staged")
        bank_ready = [sem(f"bank_ready{n}") for n in range(BANKS)]
        bank_free = [sem(f"bank_free{n}") for n in range(BANKS)]
        part_ready, last_ready = sem("part_ready"), sem("last_ready")
        out_ready, stored = sem("out_ready"), sem("stored")

        def expert_ps(t, e):
            if isinstance(t, int) and t == T - 1 and e == E - 1:
                return ring[0], 0
            return ring[e // EB], e % EB * F

        block = ctx.enter_context(nc.Block())

        def half(vector, row):
            return vec_rows[C * row:C * (row + 1), :], vector.rearrange(halves, p=P)

        @block.sync
        def _(sp):
            for i in range(PAIRS):
                sp.dma_start(x_sb[:, 2 * i:2 * i + 2, :], x_v[:, 2 * i:2 * i + 2, :]).then_inc(x_in[i], 16)
            sp.dma_start(wo_sb[:], Wo.rearrange("(c p) h -> p c h", p=P)).then_inc(wo_in, 16)
            for e in range(E):
                sp.dma_start(we_sb[:, e], We[e].rearrange("(c p) f -> p c f", p=P)).then_inc(we_in[e], 16)
            with sp.Fori(0, PAIRS - 1) as i:
                sp.wait_ge(out_ready, 2 * i + 2)
                sp.dma_start(out_v[:, bass.ds(2 * i, 2), :], out_sb[:, bass.ds(2 * i, 2), :]).then_inc(stored, 16)
            for t in (T - 2, T - 1):
                sp.wait_ge(out_ready, t + 1)
                sp.dma_start(out_v[:, t, :], out_sb[:, t, :]).then_inc(stored, 16)
            sp.wait_ge(stored, 16 * (PAIRS + 1))

        @block.gpsimd
        def _(pool):
            nc.gpsimd.memset(ones[:], 1.0).then_inc(pool_done, 1)
            nc.gpsimd.memset(warm[:].bitcast(U32), 0).then_inc(warm_ready, 1)
            nc.gpsimd.memset(eps[:], EPS)
            nc.gpsimd.memset(be_sb[:], 0.0)
            nc.gpsimd.memset(gates_3[:], 0.0).then_inc(zeros_ready, 1)
            nc.gpsimd.iota(iota_e[:], pattern=[[1, E]], base=0, channel_multiplier=0,
                           allow_small_or_imprecise_dtypes=True)
            pool.wait_ge(pool_done, 1)
            nc.gpsimd.affine_select(out=ident[:], in_=ones[:], compare_op=ALU.is_equal, fill=0.0, base=0,
                                    pattern=[[-1, P]], channel_multiplier=1)
            nc.gpsimd.affine_select(out=blk_sel[:], in_=ones[:, 0:NB], compare_op=ALU.is_ge, fill=0.0, base=0,
                                    pattern=[[-PB, NB]], channel_multiplier=1).then_inc(pool_done, 1)
            pool.wait_ge(pool_done, 2)
            nc.gpsimd.affine_select(out=blk_sel[:], in_=blk_sel[:], compare_op=ALU.is_ge, fill=0.0, base=PB - 1,
                                    pattern=[[PB, NB]], channel_multiplier=-1).then_inc(const_ready, 1)
            for row, vector in enumerate((ln_gamma, ln_beta)):
                pool.dma_start(*half(vector, row)).then_inc(affine_in, 16)
            pool.wait_ge(zeros_ready, 1)
            for q in range(3):
                pool.dma_start(be_sb[q * Q:q * Q + E, :], be).then_inc(be_in, 16)
            pool.dma_start(wr_sb[:], Wr.rearrange("(c p) e -> p c e", p=P)).then_inc(wr_in, 16)
            for e in range(E):
                if e in LO_DVE:
                    continue
                pool.wait_ge(we_hi_ready, e + 1)
                nc.gpsimd.tensor_sub(we_lo[:, e], we_sb[:, e], we_hi[:, e].bitcast(F32)).then_inc(we_lo_ready, 1)
            pool.wait_ge(proj_copied, 1)
            for t in range(2, T):
                nc.gpsimd.tensor_add(x1[:, t], x_sb[:, t], proj_sb[:]).then_inc(x1_ready, 1)

            SUMS = 4

            def sum_up(t, s, done):
                pool.wait_ge(bank_free[1], t + 1)
                nc.gpsimd.tensor_add(part[:, s, 0], stage[:, s, 0], stage[:, s, 1]).then_inc(pool_done, 1)
                pool.wait_ge(bank_free[2], t + 1)
                pool.wait_ge(pool_done, done + 1)
                nc.gpsimd.tensor_add(part[:, s, 1], acc[:, s], part[:, s, 0]).then_inc(pool_done, 1)
                pool.wait_ge(bias_staged, t + 1)
                pool.wait_ge(pool_done, done + 2)
                nc.gpsimd.tensor_add(part[:, s, 2], stage[:, s, 2], part[:, s, 1]).then_inc(pool_done, 1)
                pool.wait_ge(bank_free[3], t + 1)
                pool.wait_ge(pool_done, done + 3)
                nc.gpsimd.tensor_add(part[:, s, 3], stage[:, s, 3], part[:, s, 2]).then_inc(pool_done, 1)
                pool.wait_ge(pool_done, done + 4)
                nc.gpsimd.tensor_add(out_sb[:, t, :], stage[:, s, 4], part[:, s, 3]).then_inc(out_ready, 1)

            with pool.Fori(0, PAIRS - 1) as i:
                sum_up(2 * i, 0, 2 + SUMS * (2 * i))
                sum_up(2 * i + 1, 1, 2 + SUMS * (2 * i + 1))
            sum_up(T - 2, 0, 2 + SUMS * (T - 2))
            pool.wait_ge(bank_free[1], T)
            nc.gpsimd.tensor_add(part[:, 1, 0], stage[:, 1, 0], stage[:, 1, 1]).then_inc(pool_done, 1)
            pool.wait_ge(bias_staged, T)
            pool.wait_ge(pool_done, 2 + SUMS * (T - 1) + 1)
            nc.gpsimd.tensor_add(part[:, 1, 1], stage[:, 1, 2], part[:, 1, 0]).then_inc(part_ready, 1)

        @block.scalar
        def _(act):
            act.dma_start(wk_sb[:], Wk.rearrange("(c p) h -> p c h", p=P)).then_inc(wk_in, 16)
            for row, vector in enumerate((rms_weight, cond[LAYER])):
                act.dma_start(*half(vector, 2 + row)).then_inc(vec_in, 16)
            nc.scalar.preload_act_table_set("natural_log_exp_and_others")

            def high_weights(e):
                act.wait_ge(we_in[e], 16)
                nc.scalar.copy(we_hi[:, e], we_sb[:, e]).then_inc(we_hi_ready, 1)

            act.wait_ge(wkT_raw, 1)
            nc.scalar.activation(wkT[:].rearrange("p c h -> p (c h)"), bank[0][:], ACT.Identity).then_inc(wkT_ready, 1)
            act.wait_ge(woT_raw, 1)
            nc.scalar.activation(woT[:].rearrange("p c h -> p (c h)"), bank[1][:], ACT.Identity).then_inc(woT_ready, 1)
            high_weights(0)
            act.wait_ge(keys_ready, 1)
            nc.scalar.activation(to_sum[:, :, 0], bank[5][:, 0:C * NB].rearrange("p (c n) -> p c n", c=C),
                                 ACT.Square).then_inc(key_sq_ready, 1)
            high_weights(1)
            act.wait_ge(key_sums_ready, 1)
            nc.scalar.activation(k_ln[:], bank[6][:, 0:NB], ACT.Ln, bias=eps[:], scale=1.0 / H).then_inc(act_done, 1)
            act.wait_ge(act_done, 1)
            nc.scalar.activation(k_rstd[:], k_ln[:], ACT.Exp, scale=-0.5).then_inc(k_rstd_ready, 1)
            high_weights(2)
            act.wait_ge(score_ready, 1)
            nc.scalar.activation(prob[:], score_c[:], ACT.Exp).then_inc(prob_ready, 1)
            for e in range(3, E):
                high_weights(e)

            def rstd_start(k, t0, t1):
                act.wait_ge(var_ready, k)
                nc.scalar.activation(v_ln[:, t0:t1], mv[:, t0:t1, 1], ACT.Ln, bias=eps[:]).then_inc(act_done, 1)
                act.wait_ge(act_done, k + 1)
                nc.scalar.activation(y0[:, t0:t1], v_ln[:, t0:t1], ACT.Exp, scale=-0.5).then_inc(y0_ready, 1)

            def scale_shift(u, s):
                act.wait_ge(zT_ready, u + 1)
                if not isinstance(u, int) or u >= 2:
                    act.wait_ge(lo_ready, u - 1)
                for c in range(C):
                    last = nc.scalar.activation(h32[:, s, c], ps_zT[:, c * P:(c + 1) * P], ACT.Identity,
                                                bias=vec[:, C + c:C + c + 1], scale=vec[:, c:c + 1])
                last.then_inc(h_ready, 1)

            def second_gate(u, s):
                act.wait_ge(top_ready, u + 1)
                nc.scalar.activation(e_2nd[:, s], top_v[:, s, 0:1], ACT.Exp, bias=top_v[:, s, 1:2],
                                     scale=-1.0).then_inc(e_ready, 1)

            def copy_gatesT(t, s):
                act.wait_ge(gatesT_raw, t + 1)
                nc.scalar.activation(gatesT[:, s], ps_small[0:3 * Q, GATES_T], ACT.Identity).then_inc(gatesT_ready, 1)

            def gated(t, s, n, k):
                act.wait_ge(bank_ready[n], t + 1)
                for j in range(EB):
                    e = EB * n + j
                    last = nc.scalar.activation(stage[:, s, k + j], ring[n][:, j * F:(j + 1) * F], ACT.Copy,
                                                scale=gates[:, s, e:e + 1])
                last.then_inc(bank_free[n], 1)

            def stage_bias(t, s):
                act.wait_ge(bias_ready, t + 1)
                nc.scalar.activation(stage[:, s, 2], ps_bias[:, 0:F], ACT.Identity).then_inc(bias_staged, 1)

            act.wait_ge(x1_0_ready, 1)
            nc.scalar.activation(proj_sb[:], ps_proj[:, 0:H], ACT.Identity).then_inc(proj_copied, 1)
            rstd_start(1, 0, 1)
            act.wait_ge(vec_ready, 1)
            act.wait_ge(zT_ready, 1)
            nc.scalar.activation(h32[:, 0, 0], ps_zT[:, 0:P], ACT.Identity, bias=vec[:, C:C + 1],
                                 scale=vec[:, 0:1]).then_inc(h_ready, 1)
            rstd_start(2, 1, 2)

            def step(t, s, last):
                if not last:
                    scale_shift(t + 1, 1 - s)
                if isinstance(t, int) and t == 0:
                    second_gate(0, 0)
                    rstd_start(3, 2, 4)
                copy_gatesT(t, s)
                if not isinstance(t, int) or t >= 2:
                    act.wait_ge(out_ready, t - 1)
                gated(t, s, 1, 0)
                if isinstance(t, int) and t == 0:
                    rstd_start(4, 4, T)
                stage_bias(t, s)
                if not last:
                    second_gate(t + 1, 1 - s)
                    gated(t, s, 3, 3)

            step(0, 0, False)
            step(1, 1, False)
            with act.Fori(1, PAIRS - 1) as i:
                step(2 * i, 0, False)
                step(2 * i + 1, 1, False)
            step(T - 2, 0, False)
            step(T - 1, 1, True)

        @block.vector
        def _(dve):
            own = Counted(dve, dve_done)
            link, mark = own.link, own.mark

            dve.wait_ge(x_in[0], 16)
            dve.wait_ge(x_in[1], 16)
            link(nc.vector.tensor_add(x_pair[:, 0], x_sb[:, 0:2], x_sb[:, 2:4]))
            dve.wait_ge(x_in[2], 16)
            link(nc.vector.tensor_add(x_pair[:, 1], x_pair[:, 0], x_sb[:, 4:6]))
            dve.wait_ge(vecT_ready, 1)
            nc.vector.tensor_copy(vec[:], bank[2][:, 0:4 * C]).then_inc(vec_ready, 1)
            dve.wait_ge(vec_ready, 1)
            nc.vector.tensor_tensor(kq[:], vec[:, 2 * C:3 * C], vec[:, 3 * C:4 * C], ALU.mult).then_inc(kq_ready, 1)
            dve.wait_ge(x_in[3], 16)
            link(nc.vector.tensor_add(x_pair[:, 0], x_pair[:, 1], x_sb[:, 6:8]))
            nc.vector.tensor_add(x_sum[:], x_pair[:, 0, 0], x_pair[:, 0, 1]).then_inc(x_sum_ready, 1)
            dve.wait_ge(u_raw, 1)
            nc.vector.tensor_copy(u_sb[:], bank[2][:, 0:C]).then_inc(u_ready, 1)
            dve.wait_ge(u_ready, 1)
            dve.wait_ge(blk_raw, 1)
            nc.vector.tensor_copy(blkT[:].rearrange("p c n -> p (c n)"), bank[4][:, 0:C * NB]).then_inc(blk_ready, 1)
            dve.wait_ge(blk_ready, 1)
            for c in range(C):
                last = nc.vector.tensor_scalar(to_sum[:, c, 1], blkT[:, c], u_sb[:, c:c + 1], None, ALU.mult)
            last.then_inc(ub_ready, 1)
            dve.wait_ge(wr_in, 16)
            dve.wait_ge(be_in, 16 * 3)
            nc.vector.tensor_copy(wr_2[:, :, 0], wr_sb[:])
            link(nc.vector.tensor_copy(be_3[:], be_sb[:]))
            nc.vector.tensor_sub(wr_2[:, :, 1], wr_sb[:], wr_2[:, :, 0].bitcast(F32)).then_inc(wr_ready, 1)
            nc.vector.tensor_sub(be_3[Q:2 * Q], be_sb[Q:2 * Q], be_3[Q:2 * Q].bitcast(F32)).then_inc(be_ready, 1)
            def low_weights(e):
                dve.wait_ge(we_hi_ready, e + 1)
                nc.vector.tensor_sub(we_lo[:, e], we_sb[:, e], we_hi[:, e].bitcast(F32)).then_inc(we_lo_dve, 1)

            low_weights(LO_DVE[0])
            dve.wait_ge(k_rstd_ready, 1)
            link(nc.vector.tensor_tensor(score[:], bank[6][:, NB:2 * NB], k_rstd[:], ALU.mult))
            by_seq = "p (b n) -> p b n"
            link(nc.vector.tensor_reduce(score_max[:], score[:].rearrange(by_seq, b=B), AX_X, ALU.max))
            nc.vector.tensor_tensor(score_c[:].rearrange(by_seq, b=B), score[:].rearrange(by_seq, b=B),
                                    score_max[:].unsqueeze(2).to_broadcast([P, B, N_BLOCKS]),
                                    ALU.subtract).then_inc(score_ready, 1)
            dve.wait_ge(prob_ready, 1)
            summed = mark(nc.vector.tensor_reduce(prob_sum[:], prob[:].rearrange(by_seq, b=B), AX_X, ALU.add))
            weighed = mark(nc.vector.tensor_tensor(weighted[:], blkT[:], prob[:].unsqueeze(1).to_broadcast([P, C, NB]),
                                                   ALU.mult))
            dve.wait_ge(dve_done, summed)
            mark(nc.vector.reciprocal(prob_rec[:], prob_sum[:]))
            dve.wait_ge(dve_done, weighed)
            link(nc.vector.tensor_reduce(attended[:], weighted[:].rearrange("p c (b n) -> p c b n", b=B), AX_X, ALU.add))
            nc.vector.tensor_tensor(att_bc[:].rearrange("p c (b r) -> p c b r", b=B),
                                    attended[:].unsqueeze(3).to_broadcast([P, C, B, BP]),
                                    prob_rec[:].unsqueeze(1).unsqueeze(3).to_broadcast([P, C, B, BP]),
                                    ALU.mult).then_inc(att_ready, 1)

            def token_stats(tiles):
                for t in tiles:
                    last = nc.vector.bn_stats(stats[:, t], x1[:, t])
                link(last)
                for t in tiles:
                    last = nc.vector.bn_aggr(mv[:, t], stats[:, t])
                last.then_inc(var_ready, 1)

            def refine(k, t0, t1):
                ts = slice(t0, t1)
                dve.wait_ge(var_ready, k)
                dve.wait_ge(y0_ready, k)
                link(nc.vector.tensor_tensor(y_a[:, ts], y0[:, ts], y0[:, ts], ALU.mult))
                link(nc.vector.scalar_tensor_tensor(out=y_b[:, ts], in0=mv[:, ts, 1], scalar=EPS, in1=y_a[:, ts],
                                                    op0=ALU.add, op1=ALU.mult))
                link(nc.vector.tensor_scalar(y_c[:, ts], y_b[:, ts], -0.5, 1.5, ALU.mult, ALU.add))
                link(nc.vector.tensor_tensor(rstd[:, ts], y0[:, ts], y_c[:, ts], ALU.mult))

            def normalise(u, s):
                if not isinstance(u, int) or u >= 2:
                    dve.wait_ge(zT_ready, u - 1)
                nc.vector.tensor_scalar(z[:, s], x1[:, u], mv[:, u, 0:1], rstd[:, bass.ds(u, 1)],
                                        ALU.subtract, ALU.mult).then_inc(z_ready, 1)

            def split(u, s):
                dve.wait_ge(h_ready, u + 1)
                if isinstance(u, int) and u == 0:
                    dve.wait_ge(h0_ready, 1)
                if not isinstance(u, int) or u >= 2:
                    dve.wait_ge(bank_ready[BANKS - 1], u - 1)
                nc.vector.tensor_copy(h_hi[:, s], h32[:, s]).then_inc(hi_ready, 1)
                dve.wait_ge(hi_ready, u + 1)
                nc.vector.tensor_sub(h_lo[:, s], h32[:, s], h_hi[:, s].bitcast(F32)).then_inc(lo_ready, 1)

            def top_two(u, s):
                dve.wait_ge(logits_ready, u + 1)
                nc.vector.tensor_reduce(logits[:, s], ps_small[:, LOGITS].rearrange("p (a e) -> p e a", a=2), AX_X,
                                        ALU.add).then_inc(logits_summed, 1)
                dve.wait_ge(const_ready, 1)
                dve.wait_ge(logits_summed, u + 1)
                nc.vector.max(top_v[:, s], logits[:, s]).then_inc(top_ready, 1)
                dve.wait_ge(const_ready, 1)
                dve.wait_ge(top_ready, u + 1)
                link(nc.vector.max_index(top_i[:, s], top_v[:, s], logits[:, s]))
                nc.vector.tensor_scalar(is_1st[:, s], iota_e[:], top_i[:, s, 0:1], None, ALU.is_equal)
                return mark(nc.vector.tensor_scalar(is_2nd[:, s], iota_e[:], top_i[:, s, 1:2], None, ALU.is_equal))

            def gate(u, s, placed):
                dve.wait_ge(e_ready, u + 1)
                added = mark(nc.vector.tensor_scalar(e_den[:, s], e_2nd[:, s], 1.0, None, ALU.add))
                dve.wait_ge(dve_done, placed)
                spread = mark(nc.vector.scalar_tensor_tensor(out=e_both[:, s], in0=is_2nd[:, s], scalar=e_2nd[:, s],
                                                             in1=is_1st[:, s], op0=ALU.mult, op1=ALU.add))
                dve.wait_ge(dve_done, added)
                inverted = mark(nc.vector.reciprocal(e_rec[:, s], e_den[:, s]))
                dve.wait_ge(dve_done, inverted)
                nc.vector.tensor_scalar(gates[:, s], e_both[:, s], e_rec[:, s], None, ALU.mult).then_inc(gates_ready, 1)
                dve.wait_ge(gates_ready, u + 1)
                high = gates_3[:, s, 0:2 * Q].rearrange("p (q e) -> p q e", q=2)[:, :, 0:E]
                link(nc.vector.tensor_copy(high.bitcast(F32R), gates[:, s].unsqueeze(1).to_broadcast([P, 2, E])))
                nc.vector.tensor_sub(gates_3[:, s, 2 * Q:2 * Q + E], gates[:, s], gates_3[:, s, 0:E]).then_inc(parts_ready, 1)

            def gated_sum(t, s, e, before, to):
                ps, at = expert_ps(t, e)
                return nc.vector.scalar_tensor_tensor(out=to, in0=ps[:, at:at + F], scalar=gates[:, s, e:e + 1],
                                                      in1=before, op0=ALU.mult, op1=ALU.add)

            def add_gated(t, s, n):
                dve.wait_ge(bank_ready[n], t + 1)
                e = EB * n
                link(gated_sum(t, s, e, x_sb[:, t] if n == 0 else acc[:, s], acc[:, s]))
                gated_sum(t, s, e + 1, acc[:, s], acc[:, s]).then_inc(bank_free[n], 1)
                dve.wait_ge(bank_free[n], t + 1)

            low_weights(LO_DVE[1])
            dve.wait_ge(proj_ready, 1)
            nc.vector.tensor_add(x1[:, 0], x_sb[:, 0], ps_proj[:, 0:H]).then_inc(x1_0_ready, 1)
            dve.wait_ge(x1_0_ready, 1)
            token_stats([0])
            dve.wait_ge(proj_copied, 1)
            link(nc.vector.tensor_add(x1[:, 1], x_sb[:, 1], proj_sb[:]))
            refine(1, 0, 1)
            normalise(0, 0)
            token_stats([1])
            dve.wait_ge(zT_ready, 1)
            nc.vector.tensor_scalar(h32[:, 0, 1], bank[5][:, 0:P], vec[:, 1:2], vec[:, C + 1:C + 2], ALU.mult,
                                    ALU.add).then_inc(h0_ready, 1)
            split(0, 0)
            refine(2, 1, 2)
            normalise(1, 1)

            def step(t, s, last):
                if isinstance(t, int) and t == 0:
                    gate(0, 0, top_two(0, 0))
                if not last:
                    split(t + 1, 1 - s)
                dve.wait_ge(gates_ready, t + 1)
                if not isinstance(t, int) or t >= 2:
                    dve.wait_ge(out_ready, t - 1)
                if isinstance(t, int) and t == 0:
                    dve.wait_ge(x1_ready, 2)
                    token_stats((2, 3))
                add_gated(t, s, 0)
                if isinstance(t, int) and t == 0:
                    refine(3, 2, 4)
                    dve.wait_ge(x1_ready, T - 2)
                    token_stats(range(4, T))
                if isinstance(t, int) and t == 1:
                    refine(4, 4, T)
                if not isinstance(t, int) or t < T - 2:
                    normalise(t + 2, s)
                add_gated(t, s, 2)
                if not last:
                    gate(t + 1, 1 - s, top_two(t + 1, 1 - s))

            step(0, 0, False)
            step(1, 1, False)
            base, STEP = own.value, 8
            with dve.Fori(1, PAIRS - 1) as i:
                own.value = base + 2 * STEP * (i - 1)
                step(2 * i, 0, False)
                step(2 * i + 1, 1, False)
            own.value = base + 2 * STEP * (PAIRS - 2)
            step(T - 2, 0, False)
            assert own.value == base + 2 * STEP * (PAIRS - 2) + STEP
            step(T - 1, 1, True)
            dve.wait_ge(part_ready, 1)
            link(nc.vector.tensor_add(acc[:, 1], acc[:, 1], part[:, 1, 1]))
            dve.wait_ge(last_ready, 1)
            link(gated_sum(T - 1, 1, E - 2, acc[:, 1], acc[:, 1]))
            dve.wait_ge(last_ready, 2)
            gated_sum(T - 1, 1, E - 1, acc[:, 1], out_sb[:, T - 1]).then_inc(out_ready, 1)

        @block.tensor
        def _(pe):
            def transpose_weights(dst, w):
                for c in range(C):
                    for k in range(C):
                        last = nc.tensor.transpose(dst[:, c * H + k * P:c * H + (k + 1) * P],
                                                   w[:, k, c * P:(c + 1) * P], ident[:])
                return last

            def keep_warm(n):
                for _ in range(n):
                    nc.tensor.matmul(ring[BANKS - 1][:], warm[:, 0:P], warm[:], start=True, stop=True)

            pe.wait_ge(warm_ready, 1)
            pe.wait_ge(const_ready, 1)
            pe.wait_ge(wk_in, 16)
            transpose_weights(bank[0], wk_sb).then_inc(wkT_raw, 1)
            keep_warm(WARM[3])
            pe.wait_ge(vec_in, 16 * 2)
            pe.wait_ge(affine_in, 16 * 2)
            nc.tensor.transpose(bank[2][:, 0:4 * C], vec_rows[:], ident[0:4 * C, 0:4 * C]).then_inc(vecT_ready, 1)
            pe.wait_ge(wo_in, 16)
            transpose_weights(bank[1], wo_sb).then_inc(woT_raw, 1)
            pe.wait_ge(kq_ready, 1)
            for c in range(C):
                for k in range(C):
                    last = nc.tensor.matmul(bank[2][:, c:c + 1], wk_sb[:, k, c * P:(c + 1) * P], kq[:, k:k + 1],
                                            start=(k == 0), stop=(k == C - 1))
            last.then_inc(u_raw, 1)
            keep_warm(WARM[4])
            pe.wait_ge(x_sum_ready, 1)
            for c in range(C):
                last = nc.tensor.matmul(bank[4][:, c * NB:(c + 1) * NB], x_sum[:, c * P:(c + 1) * P], blk_sel[:],
                                        start=True, stop=True)
            last.then_inc(blk_raw, 1)
            pe.wait_ge(blk_ready, 1)
            pe.wait_ge(wkT_ready, 1)
            for k in range(C):
                for c in range(C):
                    last = nc.tensor.matmul(bank[5][:, k * NB:(k + 1) * NB], wkT[:, c, k * P:(k + 1) * P], blkT[:, c],
                                            start=(c == 0), stop=(c == C - 1))
            last.then_inc(keys_ready, 1)
            pe.wait_ge(ub_ready, 1)
            pe.wait_ge(key_sq_ready, 1)
            for c in range(C):
                last = nc.tensor.matmul(bank[6][:, 0:2 * NB], ones[:], to_sum[:, c].rearrange("p a n -> p (a n)"),
                                        start=(c == 0), stop=(c == C - 1))
            last.then_inc(key_sums_ready, 1)
            keep_warm(WARM[0])
            pe.wait_ge(woT_ready, 1)
            pe.wait_ge(att_ready, 1)
            for c in range(C):
                last = nc.tensor.matmul(ps_proj[:, 0:H], att_bc[:, c], woT[:, c], start=(c == 0), stop=(c == C - 1))
            last.then_inc(proj_ready, 1)

            def transpose_tile(u, s):
                pe.wait_ge(z_ready, u + 1)
                for c in range(C):
                    dst = bank[5][:, 0:P] if c and isinstance(u, int) and u == 0 else ps_zT[:, c * P:(c + 1) * P]
                    last = nc.tensor.transpose(dst, z[:, s, c * P:(c + 1) * P], ident[:])
                last.then_inc(zT_ready, 1)

            TERMS = 3 * C
            ROUTES = 2 * C

            def route(u, s, k):
                c, h = k // 2, (h_hi, h_lo)[k % 2]
                if k == 0:
                    pe.wait_ge(lo_ready, u + 1)
                    if not isinstance(u, int) or u >= 1:
                        pe.wait_ge(gatesT_ready, u)
                ins = nc.tensor.matmul(ps_small[:, LOGITS], h[:, s, c], wr_2[:, c].rearrange("p a e -> p (a e)"),
                                       start=(k == 0), stop=(k == ROUTES - 1))
                if k == ROUTES - 1:
                    ins.then_inc(logits_ready, 1)

            def transpose_gates(t, s):
                pe.wait_ge(parts_ready, t + 1)
                nc.tensor.transpose(ps_small[0:3 * Q, GATES_T], gates_3[:, s], ident[:]).then_inc(gatesT_raw, 1)

            def bias(t, s):
                pe.wait_ge(gatesT_ready, t + 1)
                if not isinstance(t, int) or t >= 1:
                    pe.wait_ge(bias_staged, t)
                else:
                    pe.wait_ge(be_ready, 1)
                nc.tensor.matmul(ps_bias[:, 0:F], gatesT[:, s], be_3[:], start=True, stop=True).then_inc(bias_ready, 1)

            def experts(t, s, n, between=()):
                if not isinstance(t, int) or t >= 1:
                    pe.wait_ge(bank_free[n], t)
                else:
                    es = range(EB * (n + 1))
                    pe.wait_ge(we_lo_ready, sum(e not in LO_DVE for e in es))
                    pe.wait_ge(we_lo_dve, sum(e in LO_DVE for e in es))
                terms = [(h, w, c) for c in range(C) for h, w in ((h_hi, we_hi), (h_hi, we_lo), (h_lo, we_hi))]
                for k, (h, w, c) in enumerate(terms):
                    ins = nc.tensor.matmul(ring[n][:], h[:, s, c], w[:, EB * n:EB * (n + 1), c],
                                           start=(k == 0), stop=(k == TERMS - 1))
                    if k == TERMS - 1:
                        ins.then_inc(bank_ready[n], 1)
                    for at, issue in between:
                        if at == k:
                            issue()

            def routing(u, s, k0):
                return [(k0 + k, lambda k=k: route(u, s, k)) for k in range(ROUTES)]

            def last_experts(t, s):
                pe.wait_ge(bank_free[BANKS - 1], t)
                pe.wait_ge(bank_free[0], t + 1)
                for e in (E - 2, E - 1):
                    ps, at = expert_ps(t, e)
                    terms = [(h, w, c) for c in range(C) for h, w in ((h_hi, we_hi), (h_hi, we_lo), (h_lo, we_hi))]
                    for k, (h, w, c) in enumerate(terms):
                        ins = nc.tensor.matmul(ps[:, at:at + F], h[:, s, c], w[:, e, c],
                                               start=(k == 0), stop=(k == TERMS - 1))
                    ins.then_inc(last_ready, 1)

            def step(t, s, last):
                first = isinstance(t, int) and t == 0
                next_tile = (2, lambda: transpose_tile(t + 1, 1 - s))
                turn_gates = (3, lambda: transpose_gates(t, s))
                if first:
                    for k in range(ROUTES):
                        route(0, 0, k)
                    experts(0, 0, 0, [next_tile])
                    experts(0, 0, 1)
                    experts(0, 0, 2, [turn_gates])
                    experts(0, 0, 3, routing(1, 1, 0) + [(TERMS - 1, lambda: bias(0, 0))])
                elif last:
                    experts(t, s, 0)
                    experts(t, s, 1, [turn_gates])
                    experts(t, s, 2, [(2, lambda: bias(t, s))])
                    last_experts(t, s)
                else:
                    experts(t, s, 0, [next_tile])
                    experts(t, s, 1, [turn_gates])
                    experts(t, s, 2, routing(t + 1, 1 - s, 1))
                    experts(t, s, 3, [(1, lambda: bias(t, s))])

            keep_warm(WARM[1])
            transpose_tile(0, 0)
            pe.wait_ge(wr_ready, 1)
            keep_warm(WARM[2])
            pe.wait_ge(lo_ready, 1)
            step(0, 0, False)
            step(1, 1, False)
            with pe.Fori(1, PAIRS - 1) as i:
                step(2 * i, 0, False)
                step(2 * i + 1, 1, False)
            step(T - 2, 0, False)
            step(T - 1, 1, True)


_INS = ['x', 'cond_2048', 'L0_cond_rms_weight', 'L0_cond_Wk', 'L0_cond_Wo', 'L0_cond_ln_gamma', 'L0_cond_ln_beta',
        'L0_ffn_Wr', 'L0_ffn_We', 'L0_ffn_be']
_OUTS = [((4, 256, 256), 'float32')]


def kernel(**inputs):
    import numpy as _np
    import concourse.bacc as _bacc
    from concourse import mybir as _mybir
    from concourse.bass_utils import run_bass_kernel_spmd as _run

    nc = _bacc.Bacc("TRN2", target_bir_lowering=False, num_devices=1)
    arrays, args = {}, []
    for name in _INS:
        a = _np.ascontiguousarray(inputs[name])
        arrays[f"in_{name}_dram"] = a
        args.append(nc.dram_tensor(f"in_{name}_dram", a.shape, _mybir.dt.from_np(a.dtype), kind="ExternalInput").ap())
    for i, (shape, dtype) in enumerate(_OUTS):
        dt = _mybir.dt.from_np(_np.dtype(dtype))
        args.append(nc.dram_tensor(f"out_{i}_dram", shape, dt, kind="ExternalOutput").ap())
    adaln_ffn_kernel(nc, *args)
    r = _run(nc, [arrays], core_ids=[0])
    got = tuple(r.results[0][f"out_{i}_dram"] for i in range(len(_OUTS)))
    return got[0]
```

```python
from contextlib import ExitStack

import concourse.bass as bass
from concourse import mybir

P = 128
F32 = mybir.dt.float32
F32R = mybir.dt.float32r
BF16 = mybir.dt.bfloat16
U32 = mybir.dt.uint32
ALU = mybir.AluOpType
ACT = mybir.ActivationFunctionType
AX_X = mybir.AxisListType.X


class Counted:

    def __init__(self, engine, semaphore):
        self.engine, self.semaphore, self.value = engine, semaphore, 0

    def mark(self, instruction):
        instruction.then_inc(self.semaphore, 1)
        self.value = self.value + 1
        return self.value

    def link(self, instruction):
        self.engine.wait_ge(self.semaphore, self.mark(instruction))


def adaln_ffn_kernel(
    nc: bass.Bass,
    x: bass.AP,
    cond: bass.AP,
    rms_weight: bass.AP,
    Wk: bass.AP,
    Wo: bass.AP,
    ln_gamma: bass.AP,
    ln_beta: bass.AP,
    Wr: bass.AP,
    We: bass.AP,
    be: bass.AP,
    out: bass.AP,
):
    B, S, H = x.shape
    E, _, F = We.shape
    N_BLOCKS = 8
    LAYER = 1
    EPS = 1e-6
    T = B * S // P
    C = H // P
    NB = B * N_BLOCKS
    PB = P // NB
    BP = P // B
    BANKS = E * F // 512
    EB = E // BANKS
    PAIRS = T // 2
    LO_DVE = (0,)
    WARM = (5, 11, 4, 1, 1)
    Q = 32
    assert C == 2 and F == 256 and BANKS == 4 and EB == 2 and T == 8

    x_v = x.rearrange("b s h -> (b s) h").rearrange("(p t) h -> p t h", t=T)
    out_v = out.rearrange("b s h -> (b s) h").rearrange("(p t) h -> p t h", t=T)
    halves = "(c p) -> c p"

    ctx = ExitStack()
    with ctx:
        def sb(name, shape, dt=F32):
            return ctx.enter_context(nc.sbuf_tensor(name, shape, dt))

        def sem(name):
            return ctx.enter_context(nc.semaphore(name))

        x_sb = sb("x_sb", [P, T, H])
        x1 = sb("x1", [P, T, H])
        out_sb = sb("out_sb", [P, T, F])
        wk_sb = sb("wk_sb", [P, C, H])
        wo_sb = sb("wo_sb", [P, C, H])
        wkT = sb("wkT", [P, C, H])
        woT = sb("woT", [P, C, H])
        key_rows = sb("key_rows", [2 * C, P])
        key_vec = sb("key_vec", [P, 2 * C])
        affine_rows = sb("affine_rows", [2 * C, P])
        affine = sb("affine", [P, 2 * C])
        kq = sb("kq", [P, C])
        u_sb = sb("u_sb", [P, C])
        x_pair = sb("x_pair", [P, 2, 2, H])
        x_sum = sb("x_sum", [P, H])
        blkT = sb("blkT", [P, C, NB])
        to_sum = sb("to_sum", [P, C, 2, NB])
        proj_sb = sb("proj_sb", [P, H])
        k_ln = sb("k_ln", [P, NB])
        k_rstd = sb("k_rstd", [P, NB])
        score = sb("score", [P, NB])
        score_max = sb("score_max", [P, B])
        score_c = sb("score_c", [P, NB])
        prob = sb("prob", [P, NB])
        prob_sum = sb("prob_sum", [P, B])
        prob_rec = sb("prob_rec", [P, B])
        weighted = sb("weighted", [P, C, NB])
        attended = sb("attended", [P, C, B])
        att_bc = sb("att_bc", [P, C, P])
        ident = sb("ident", [P, P])
        ones = sb("ones", [P, P])
        blk_sel = sb("blk_sel", [P, NB])
        iota_e = sb("iota_e", [P, E])
        eps = sb("eps", [P, 1])
        stats = sb("stats", [P, T, 6])
        mv = sb("mv", [P, T, 2])
        v_ln = sb("v_ln", [P, T])
        y0 = sb("y0", [P, T])
        v_half = sb("v_half", [P, T])
        y_a = sb("y_a", [P, T])
        y_b = sb("y_b", [P, T])
        rstd = sb("rstd", [P, T])
        z = sb("z", [P, 2, H])
        h32 = sb("h32", [P, 2, C, P])
        h_hi = sb("h_hi", [P, 2, C, P], F32R)
        h_lo = sb("h_lo", [P, 2, C, P], F32R)
        we_sb = sb("we_sb", [P, E, C, F])
        we_hi = sb("we_hi", [P, E, C, F], F32R)
        we_lo = sb("we_lo", [P, E, C, F], F32R)
        wr_sb = sb("wr_sb", [P, C, E])
        wr_2 = sb("wr_2", [P, C, 2, E], F32R)
        be_sb = sb("be_sb", [3 * Q, F])
        be_3 = sb("be_3", [3 * Q, F], F32R)
        logits = sb("logits", [P, 2, E])
        warm = sb("warm", [P, 512], BF16)
        top_v = sb("top_v", [P, 2, 8])
        top_i = sb("top_i", [P, 2, 8], U32)
        is_1st = sb("is_1st", [P, 2, E])
        is_2nd = sb("is_2nd", [P, 2, E])
        e_2nd = sb("e_2nd", [P, 2, 1])
        e_den = sb("e_den", [P, 2, 1])
        e_rec = sb("e_rec", [P, 2, 1])
        e_both = sb("e_both", [P, 2, E])
        gates = sb("gates", [P, 2, E])
        gates_3 = sb("gates_3", [P, 2, 3 * Q])
        gatesT = sb("gatesT", [3 * Q, 2, P], F32R)
        acc = sb("acc", [P, 2, F])
        stage = sb("stage", [P, 2, 5, F])
        part = sb("part", [P, 2, 4, F])

        bank = [ctx.enter_context(nc.psum_tensor(f"bank{n}", [P, 512], F32)) for n in range(8)]
        ring = bank[0:BANKS]
        ps_zT, ps_bias, ps_small, ps_proj = bank[4], bank[5], bank[6], bank[7]
        LOGITS, GATES_T = slice(0, 2 * E), slice(P, 2 * P)

        x_in = [sem(f"x_in{i}") for i in range(PAIRS)]
        wk_in, wo_in, key_in, wr_in, be_in = (sem("wk_in"), sem("wo_in"), sem("key_in"), sem("wr_in"),
                                             sem("be_in"))
        affine_in = sem("affine_in")
        we_in = [sem(f"we_in{e}") for e in range(E)]
        const_ready = sem("const_ready")
        pool_done, dve_done, act_done = sem("pool_done"), sem("dve_done"), sem("act_done")
        key_vec_raw, key_vec_ready = sem("key_vec_raw"), sem("key_vec_ready")
        affine_raw, affine_ready = sem("affine_raw"), sem("affine_ready")
        wkT_raw, wkT_ready = sem("wkT_raw"), sem("wkT_ready")
        woT_raw, woT_ready = sem("woT_raw"), sem("woT_ready")
        kq_ready, u_raw, u_ready = sem("kq_ready"), sem("u_raw"), sem("u_ready")
        x_sum_ready, blk_raw, blk_ready = sem("x_sum_ready"), sem("blk_raw"), sem("blk_ready")
        keys_ready, key_sq_ready, ub_ready, key_sums_ready = (
            sem("keys_ready"), sem("key_sq_ready"), sem("ub_ready"), sem("key_sums_ready"))
        x1_0_ready, proj_copied, x1_ready = sem("x1_0_ready"), sem("proj_copied"), sem("x1_ready")
        h0_chunk1_ready, zeros_ready, be_ready = sem("h0_chunk1_ready"), sem("zeros_ready"), sem("be_ready")
        warm_ready, logits_summed = sem("warm_ready"), sem("logits_summed")
        k_rstd_ready, score_ready, prob_ready = sem("k_rstd_ready"), sem("score_ready"), sem("prob_ready")
        att_ready, proj_ready = sem("att_ready"), sem("proj_ready")
        var_ready, y0_ready = sem("var_ready"), sem("y0_ready")
        wr_ready, we_hi_ready, we_lo_ready, we_lo_dve = (
            sem("wr_ready"), sem("we_hi_ready"), sem("we_lo_ready"), sem("we_lo_dve"))
        z_ready, zT_ready, h_ready = sem("z_ready"), sem("zT_ready"), sem("h_ready")
        hi_ready, lo_ready = sem("hi_ready"), sem("lo_ready")
        logits_ready, top_ready, e_ready, gates_ready = (
            sem("logits_ready"), sem("top_ready"), sem("e_ready"), sem("gates_ready"))
        parts_ready = sem("parts_ready")
        gatesT_raw, gatesT_ready = sem("gatesT_raw"), sem("gatesT_ready")
        bias_ready, bias_staged = sem("bias_ready"), sem("bias_staged")
        bank_ready = [sem(f"bank_ready{n}") for n in range(BANKS)]
        bank_free = [sem(f"bank_free{n}") for n in range(BANKS)]
        last_ready, last_summed = sem("last_ready"), sem("last_summed")
        out_ready, stored = sem("out_ready"), sem("stored")

        def expert_ps(t, e):
            if isinstance(t, int) and t == T - 1 and e == E - 1:
                return ring[0], 0
            return ring[e // EB], e % EB * F

        block = ctx.enter_context(nc.Block())

        def half(rows, vector, k):
            return rows[C * k:C * (k + 1), :], vector.rearrange(halves, p=P)

        @block.sync
        def _(sp):
            for i in range(PAIRS):
                sp.dma_start(x_sb[:, 2 * i:2 * i + 2, :], x_v[:, 2 * i:2 * i + 2, :]).then_inc(x_in[i], 16)
            sp.dma_start(wo_sb[:], Wo.rearrange("(c p) h -> p c h", p=P)).then_inc(wo_in, 16)
            for e in range(E):
                sp.dma_start(we_sb[:, e], We[e].rearrange("(c p) f -> p c f", p=P)).then_inc(we_in[e], 16)
            with sp.Fori(0, PAIRS - 1) as i:
                sp.wait_ge(out_ready, 2 * i + 2)
                sp.dma_start(out_v[:, bass.ds(2 * i, 2), :], out_sb[:, bass.ds(2 * i, 2), :]).then_inc(stored, 16)
            for t, summed, count in ((T - 2, out_ready, T - 1), (T - 1, last_summed, 1)):
                sp.wait_ge(summed, count)
                sp.dma_start(out_v[:, t, :], out_sb[:, t, :]).then_inc(stored, 16)
            sp.wait_ge(stored, 16 * (PAIRS + 1))

        @block.gpsimd
        def _(pool):
            nc.gpsimd.memset(ones[:], 1.0).then_inc(pool_done, 1)
            nc.gpsimd.memset(warm[:].bitcast(U32), 0).then_inc(warm_ready, 1)
            nc.gpsimd.memset(eps[:], EPS)
            nc.gpsimd.memset(be_sb[:], 0.0)
            nc.gpsimd.memset(gates_3[:], 0.0).then_inc(zeros_ready, 1)
            nc.gpsimd.iota(iota_e[:], pattern=[[1, E]], base=0, channel_multiplier=0,
                           allow_small_or_imprecise_dtypes=True)
            pool.wait_ge(pool_done, 1)
            nc.gpsimd.affine_select(out=ident[:], in_=ones[:], compare_op=ALU.is_equal, fill=0.0, base=0,
                                    pattern=[[-1, P]], channel_multiplier=1)
            nc.gpsimd.affine_select(out=blk_sel[:], in_=ones[:, 0:NB], compare_op=ALU.is_ge, fill=0.0, base=0,
                                    pattern=[[-PB, NB]], channel_multiplier=1).then_inc(pool_done, 1)
            pool.wait_ge(pool_done, 2)
            nc.gpsimd.affine_select(out=blk_sel[:], in_=blk_sel[:], compare_op=ALU.is_ge, fill=0.0, base=PB - 1,
                                    pattern=[[PB, NB]], channel_multiplier=-1).then_inc(const_ready, 1)
            for row, vector in enumerate((ln_gamma, ln_beta)):
                pool.dma_start(*half(affine_rows, vector, row)).then_inc(affine_in, 16)
            pool.wait_ge(zeros_ready, 1)
            for q in range(3):
                pool.dma_start(be_sb[q * Q:q * Q + E, :], be).then_inc(be_in, 16)
            pool.dma_start(wr_sb[:], Wr.rearrange("(c p) e -> p c e", p=P)).then_inc(wr_in, 16)
            for e in range(E):
                if e in LO_DVE:
                    continue
                pool.wait_ge(we_hi_ready, e + 1)
                nc.gpsimd.tensor_sub(we_lo[:, e], we_sb[:, e], we_hi[:, e].bitcast(F32)).then_inc(we_lo_ready, 1)
            pool.wait_ge(proj_copied, 1)
            for t in range(2, T):
                nc.gpsimd.tensor_add(x1[:, t], x_sb[:, t], proj_sb[:]).then_inc(x1_ready, 1)

            SUMS = 4

            def sum_up(t, s, done):
                pool.wait_ge(bank_free[1], t + 1)
                nc.gpsimd.tensor_add(part[:, s, 0], stage[:, s, 0], stage[:, s, 1]).then_inc(pool_done, 1)
                pool.wait_ge(bank_free[2], t + 1)
                pool.wait_ge(pool_done, done + 1)
                nc.gpsimd.tensor_add(part[:, s, 1], acc[:, s], part[:, s, 0]).then_inc(pool_done, 1)
                pool.wait_ge(bias_staged, t + 1)
                pool.wait_ge(pool_done, done + 2)
                nc.gpsimd.tensor_add(part[:, s, 2], stage[:, s, 2], part[:, s, 1]).then_inc(pool_done, 1)
                pool.wait_ge(bank_free[3], t + 1)
                pool.wait_ge(pool_done, done + 3)
                nc.gpsimd.tensor_add(part[:, s, 3], stage[:, s, 3], part[:, s, 2]).then_inc(pool_done, 1)
                pool.wait_ge(pool_done, done + 4)
                nc.gpsimd.tensor_add(out_sb[:, t, :], stage[:, s, 4], part[:, s, 3]).then_inc(out_ready, 1)

            with pool.Fori(0, PAIRS - 1) as i:
                sum_up(2 * i, 0, 2 + SUMS * (2 * i))
                sum_up(2 * i + 1, 1, 2 + SUMS * (2 * i + 1))
            sum_up(T - 2, 0, 2 + SUMS * (T - 2))

        @block.scalar
        def _(act):
            act.dma_start(wk_sb[:], Wk.rearrange("(c p) h -> p c h", p=P)).then_inc(wk_in, 16)
            for row, vector in enumerate((rms_weight, cond[LAYER])):
                act.dma_start(*half(key_rows, vector, row)).then_inc(key_in, 16)
            nc.scalar.preload_act_table_set("natural_log_exp_and_others")

            def high_weights(e):
                act.wait_ge(we_in[e], 16)
                nc.scalar.copy(we_hi[:, e], we_sb[:, e]).then_inc(we_hi_ready, 1)

            act.wait_ge(wkT_raw, 1)
            nc.scalar.activation(wkT[:].rearrange("p c h -> p (c h)"), bank[0][:], ACT.Identity).then_inc(wkT_ready, 1)
            high_weights(0)
            high_weights(1)
            high_weights(2)
            act.wait_ge(keys_ready, 1)
            nc.scalar.activation(to_sum[:, :, 0], bank[5][:, 0:C * NB].rearrange("p (c n) -> p c n", c=C),
                                 ACT.Square).then_inc(key_sq_ready, 1)
            act.wait_ge(key_sums_ready, 1)
            nc.scalar.activation(k_ln[:], bank[6][:, 0:NB], ACT.Ln, bias=eps[:], scale=1.0 / H).then_inc(act_done, 1)
            act.wait_ge(act_done, 1)
            nc.scalar.activation(k_rstd[:], k_ln[:], ACT.Exp, scale=-0.5).then_inc(k_rstd_ready, 1)
            act.wait_ge(score_ready, 1)
            nc.scalar.activation(prob[:], score_c[:], ACT.Exp).then_inc(prob_ready, 1)
            act.wait_ge(woT_raw, 1)
            nc.scalar.activation(woT[:].rearrange("p c h -> p (c h)"), bank[1][:], ACT.Identity).then_inc(woT_ready, 1)
            for e in range(3, E):
                high_weights(e)

            def rstd_start(k, t0, t1):
                act.wait_ge(var_ready, k)
                nc.scalar.activation(v_ln[:, t0:t1], mv[:, t0:t1, 1], ACT.Ln, bias=eps[:]).then_inc(act_done, 1)
                act.wait_ge(act_done, k + 1)
                nc.scalar.activation(y0[:, t0:t1], v_ln[:, t0:t1], ACT.Exp, scale=-0.5).then_inc(y0_ready, 1)

            def scale_shift(u, s):
                act.wait_ge(zT_ready, u + 1)
                if not isinstance(u, int) or u >= 2:
                    act.wait_ge(lo_ready, u - 1)
                for c in range(C):
                    last = nc.scalar.activation(h32[:, s, c], ps_zT[:, c * P:(c + 1) * P], ACT.Identity,
                                                bias=affine[:, C + c:C + c + 1], scale=affine[:, c:c + 1])
                last.then_inc(h_ready, 1)

            def second_gate(u, s):
                act.wait_ge(top_ready, u + 1)
                nc.scalar.activation(e_2nd[:, s], top_v[:, s, 0:1], ACT.Exp, bias=top_v[:, s, 1:2],
                                     scale=-1.0).then_inc(e_ready, 1)

            def copy_gatesT(t, s):
                act.wait_ge(gatesT_raw, t + 1)
                nc.scalar.activation(gatesT[:, s], ps_small[0:3 * Q, GATES_T], ACT.Identity).then_inc(gatesT_ready, 1)

            def gated(t, s, n, k):
                act.wait_ge(bank_ready[n], t + 1)
                for j in range(EB):
                    e = EB * n + j
                    last = nc.scalar.activation(stage[:, s, k + j], ring[n][:, j * F:(j + 1) * F], ACT.Copy,
                                                scale=gates[:, s, e:e + 1])
                last.then_inc(bank_free[n], 1)

            def stage_bias(t, s):
                act.wait_ge(bias_ready, t + 1)
                nc.scalar.activation(stage[:, s, 2], ps_bias[:, 0:F], ACT.Identity).then_inc(bias_staged, 1)

            act.wait_ge(x1_0_ready, 1)
            nc.scalar.activation(proj_sb[:], ps_proj[:, 0:H], ACT.Identity).then_inc(proj_copied, 1)
            rstd_start(1, 0, 1)
            act.wait_ge(affine_ready, 1)
            act.wait_ge(zT_ready, 1)
            nc.scalar.activation(h32[:, 0, 0], ps_zT[:, 0:P], ACT.Identity, bias=affine[:, C:C + 1],
                                 scale=affine[:, 0:1]).then_inc(h_ready, 1)
            rstd_start(2, 1, 2)

            def step(t, s):
                scale_shift(t + 1, 1 - s)
                if isinstance(t, int) and t == 0:
                    second_gate(0, 0)
                if isinstance(t, int) and t == 0:
                    rstd_start(3, 2, 4)
                copy_gatesT(t, s)
                if not isinstance(t, int) or t >= 2:
                    act.wait_ge(out_ready, t - 1)
                gated(t, s, 1, 0)
                if isinstance(t, int) and t == 1:
                    rstd_start(4, 4, T)
                stage_bias(t, s)
                second_gate(t + 1, 1 - s)
                gated(t, s, 3, 3)

            step(0, 0)
            step(1, 1)
            with act.Fori(1, PAIRS - 1) as i:
                step(2 * i, 0)
                step(2 * i + 1, 1)
            step(T - 2, 0)
            copy_gatesT(T - 1, 1)

        @block.vector
        def _(dve):
            own = Counted(dve, dve_done)
            link, mark = own.link, own.mark

            dve.wait_ge(x_in[0], 16)
            dve.wait_ge(x_in[1], 16)
            link(nc.vector.tensor_add(x_pair[:, 0], x_sb[:, 0:2], x_sb[:, 2:4]))
            dve.wait_ge(x_in[2], 16)
            link(nc.vector.tensor_add(x_pair[:, 1], x_pair[:, 0], x_sb[:, 4:6]))
            dve.wait_ge(key_vec_raw, 1)
            nc.vector.tensor_copy(key_vec[:], bank[2][:, 0:2 * C]).then_inc(key_vec_ready, 1)
            dve.wait_ge(key_vec_ready, 1)
            nc.vector.tensor_tensor(kq[:], key_vec[:, 0:C], key_vec[:, C:2 * C], ALU.mult).then_inc(kq_ready, 1)
            dve.wait_ge(x_in[3], 16)
            link(nc.vector.tensor_add(x_pair[:, 0], x_pair[:, 1], x_sb[:, 6:8]))
            nc.vector.tensor_add(x_sum[:], x_pair[:, 0, 0], x_pair[:, 0, 1]).then_inc(x_sum_ready, 1)
            dve.wait_ge(blk_raw, 1)
            nc.vector.tensor_copy(blkT[:].rearrange("p c n -> p (c n)"), bank[4][:, 0:C * NB]).then_inc(blk_ready, 1)
            dve.wait_ge(u_raw, 1)
            nc.vector.tensor_copy(u_sb[:], bank[2][:, 0:C]).then_inc(u_ready, 1)
            dve.wait_ge(blk_ready, 1)
            dve.wait_ge(u_ready, 1)
            for c in range(C):
                last = nc.vector.tensor_scalar(to_sum[:, c, 1], blkT[:, c], u_sb[:, c:c + 1], None, ALU.mult)
            last.then_inc(ub_ready, 1)
            dve.wait_ge(affine_raw, 1)
            nc.vector.tensor_copy(affine[:], bank[7][:, 0:2 * C]).then_inc(affine_ready, 1)

            def low_weights(e):
                dve.wait_ge(we_hi_ready, e + 1)
                nc.vector.tensor_sub(we_lo[:, e], we_sb[:, e], we_hi[:, e].bitcast(F32)).then_inc(we_lo_dve, 1)

            for e in LO_DVE:
                low_weights(e)
            dve.wait_ge(k_rstd_ready, 1)
            link(nc.vector.tensor_tensor(score[:], bank[6][:, NB:2 * NB], k_rstd[:], ALU.mult))
            by_seq = "p (b n) -> p b n"
            link(nc.vector.tensor_reduce(score_max[:], score[:].rearrange(by_seq, b=B), AX_X, ALU.max))
            nc.vector.tensor_tensor(score_c[:].rearrange(by_seq, b=B), score[:].rearrange(by_seq, b=B),
                                    score_max[:].unsqueeze(2).to_broadcast([P, B, N_BLOCKS]),
                                    ALU.subtract).then_inc(score_ready, 1)
            dve.wait_ge(prob_ready, 1)
            summed = mark(nc.vector.tensor_reduce(prob_sum[:], prob[:].rearrange(by_seq, b=B), AX_X, ALU.add))
            weighed = mark(nc.vector.tensor_tensor(weighted[:], blkT[:], prob[:].unsqueeze(1).to_broadcast([P, C, NB]),
                                                   ALU.mult))
            dve.wait_ge(dve_done, summed)
            mark(nc.vector.reciprocal(prob_rec[:], prob_sum[:]))
            dve.wait_ge(dve_done, weighed)
            link(nc.vector.tensor_reduce(attended[:], weighted[:].rearrange("p c (b n) -> p c b n", b=B), AX_X, ALU.add))
            nc.vector.tensor_tensor(att_bc[:].rearrange("p c (b r) -> p c b r", b=B),
                                    attended[:].unsqueeze(3).to_broadcast([P, C, B, BP]),
                                    prob_rec[:].unsqueeze(1).unsqueeze(3).to_broadcast([P, C, B, BP]),
                                    ALU.mult).then_inc(att_ready, 1)

            def measure(tiles):
                for t in tiles:
                    last = nc.vector.bn_stats(stats[:, t], x1[:, t])
                return last

            def token_stats(k, tiles, rest=None):
                link(measure(rest or tiles))
                for t in tiles:
                    last = nc.vector.bn_aggr(mv[:, t], stats[:, t])
                last.then_inc(var_ready, 1)
                ts = slice(tiles[0], tiles[-1] + 1)
                dve.wait_ge(var_ready, k)
                mark(nc.vector.tensor_scalar(v_half[:, ts], mv[:, ts, 1], EPS, -0.5, ALU.add, ALU.mult))

            def refine(k, t0, t1):
                ts = slice(t0, t1)
                dve.wait_ge(y0_ready, k)
                link(nc.vector.tensor_tensor(y_a[:, ts], y0[:, ts], y0[:, ts], ALU.mult))
                link(nc.vector.tensor_tensor(y_b[:, ts], v_half[:, ts], y_a[:, ts], ALU.mult))
                link(nc.vector.scalar_tensor_tensor(out=rstd[:, ts], in0=y_b[:, ts], scalar=1.5, in1=y0[:, ts],
                                                    op0=ALU.add, op1=ALU.mult))

            def normalise(u, s):
                if not isinstance(u, int) or u >= 2:
                    dve.wait_ge(zT_ready, u - 1)
                nc.vector.tensor_scalar(z[:, s], x1[:, u], mv[:, u, 0:1], rstd[:, bass.ds(u, 1)],
                                        ALU.subtract, ALU.mult).then_inc(z_ready, 1)

            def split(u, s):
                dve.wait_ge(h_ready, u + 1)
                if isinstance(u, int) and u == 0:
                    dve.wait_ge(h0_chunk1_ready, 1)
                if not isinstance(u, int) or u >= 2:
                    dve.wait_ge(bank_ready[BANKS - 1], u - 1)
                nc.vector.tensor_copy(h_hi[:, s], h32[:, s]).then_inc(hi_ready, 1)
                dve.wait_ge(hi_ready, u + 1)
                nc.vector.tensor_sub(h_lo[:, s], h32[:, s], h_hi[:, s].bitcast(F32)).then_inc(lo_ready, 1)

            def top_two(u, s):
                dve.wait_ge(logits_ready, u + 1)
                nc.vector.tensor_reduce(logits[:, s], ps_small[:, LOGITS].rearrange("p (a e) -> p e a", a=2), AX_X,
                                        ALU.add).then_inc(logits_summed, 1)
                dve.wait_ge(const_ready, 1)
                dve.wait_ge(logits_summed, u + 1)
                nc.vector.max(top_v[:, s], logits[:, s]).then_inc(top_ready, 1)
                dve.wait_ge(const_ready, 1)
                dve.wait_ge(top_ready, u + 1)
                link(nc.vector.max_index(top_i[:, s], top_v[:, s], logits[:, s]))
                nc.vector.tensor_scalar(is_1st[:, s], iota_e[:], top_i[:, s, 0:1], None, ALU.is_equal)
                return mark(nc.vector.tensor_scalar(is_2nd[:, s], iota_e[:], top_i[:, s, 1:2], None, ALU.is_equal))

            def gate(u, s, placed):
                dve.wait_ge(e_ready, u + 1)
                added = mark(nc.vector.tensor_scalar(e_den[:, s], e_2nd[:, s], 1.0, None, ALU.add))
                dve.wait_ge(dve_done, placed)
                spread = mark(nc.vector.scalar_tensor_tensor(out=e_both[:, s], in0=is_2nd[:, s], scalar=e_2nd[:, s],
                                                             in1=is_1st[:, s], op0=ALU.mult, op1=ALU.add))
                dve.wait_ge(dve_done, added)
                inverted = mark(nc.vector.reciprocal(e_rec[:, s], e_den[:, s]))
                dve.wait_ge(dve_done, inverted)
                nc.vector.tensor_scalar(gates[:, s], e_both[:, s], e_rec[:, s], None, ALU.mult).then_inc(gates_ready, 1)
                dve.wait_ge(gates_ready, u + 1)
                high = gates_3[:, s, 0:2 * Q].rearrange("p (q e) -> p q e", q=2)[:, :, 0:E]
                link(nc.vector.tensor_copy(high.bitcast(F32R), gates[:, s].unsqueeze(1).to_broadcast([P, 2, E])))
                nc.vector.tensor_sub(gates_3[:, s, 2 * Q:2 * Q + E], gates[:, s], gates_3[:, s, 0:E]).then_inc(parts_ready, 1)

            def gated_sum(t, s, e, before, to):
                ps, at = expert_ps(t, e)
                return nc.vector.scalar_tensor_tensor(out=to, in0=ps[:, at:at + F], scalar=gates[:, s, e:e + 1],
                                                      in1=before, op0=ALU.mult, op1=ALU.add)

            def add_gated(t, s, n):
                dve.wait_ge(bank_ready[n], t + 1)
                e = EB * n
                link(gated_sum(t, s, e, x_sb[:, t] if n == 0 else acc[:, s], acc[:, s]))
                gated_sum(t, s, e + 1, acc[:, s], acc[:, s]).then_inc(bank_free[n], 1)
                dve.wait_ge(bank_free[n], t + 1)

            dve.wait_ge(wr_in, 16)
            dve.wait_ge(be_in, 16 * 3)
            nc.vector.tensor_copy(wr_2[:, :, 0], wr_sb[:])
            link(nc.vector.tensor_copy(be_3[:], be_sb[:]))
            nc.vector.tensor_sub(wr_2[:, :, 1], wr_sb[:], wr_2[:, :, 0].bitcast(F32)).then_inc(wr_ready, 1)
            nc.vector.tensor_sub(be_3[Q:2 * Q], be_sb[Q:2 * Q], be_3[Q:2 * Q].bitcast(F32)).then_inc(be_ready, 1)
            dve.wait_ge(proj_ready, 1)
            nc.vector.tensor_add(x1[:, 0], x_sb[:, 0], ps_proj[:, 0:H]).then_inc(x1_0_ready, 1)
            dve.wait_ge(x1_0_ready, 1)
            token_stats(1, [0])
            dve.wait_ge(proj_copied, 1)
            link(nc.vector.tensor_add(x1[:, 1], x_sb[:, 1], proj_sb[:]))
            refine(1, 0, 1)
            normalise(0, 0)
            token_stats(2, [1])
            dve.wait_ge(zT_ready, 1)
            nc.vector.tensor_scalar(h32[:, 0, 1], bank[5][:, 0:P], affine[:, 1:2], affine[:, C + 1:C + 2], ALU.mult,
                                    ALU.add).then_inc(h0_chunk1_ready, 1)
            split(0, 0)
            refine(2, 1, 2)
            normalise(1, 1)

            def step(t, s, last):
                first, second = (isinstance(t, int) and t == n for n in (0, 1))
                if first:
                    placed = top_two(0, 0)
                    dve.wait_ge(x1_ready, 2)
                    token_stats(3, (2, 3))
                    gate(0, 0, placed)
                if not last:
                    split(t + 1, 1 - s)
                if first:
                    refine(3, 2, 4)
                    normalise(2, 0)
                if second:
                    dve.wait_ge(x1_ready, T - 2)
                    token_stats(4, range(4, T), (T - 2, T - 1))
                dve.wait_ge(gates_ready, t + 1)
                if not isinstance(t, int) or t >= 2:
                    dve.wait_ge(out_ready, t - 1)
                add_gated(t, s, 0)
                if not first and (not isinstance(t, int) or t < T - 2):
                    normalise(t + 2, s)
                if last:
                    add_gated(t, s, 1)
                    dve.wait_ge(bias_ready, T)
                    link(nc.vector.tensor_add(acc[:, s], acc[:, s], ps_bias[:, 0:F]))
                if not last:
                    placed = top_two(t + 1, 1 - s)
                if first:
                    gate(1, 1, placed)
                add_gated(t, s, 2)
                if not last and not first:
                    gate(t + 1, 1 - s, placed)
                if first:
                    dve.wait_ge(x1_ready, 4)
                    measure((4, 5))
                if second:
                    refine(4, 4, T)

            step(0, 0, False)
            step(1, 1, False)
            base, STEP = own.value, 8
            with dve.Fori(1, PAIRS - 1) as i:
                own.value = base + 2 * STEP * (i - 1)
                step(2 * i, 0, False)
                step(2 * i + 1, 1, False)
            own.value = base + 2 * STEP * (PAIRS - 2)
            step(T - 2, 0, False)
            assert own.value == base + 2 * STEP * (PAIRS - 2) + STEP
            step(T - 1, 1, True)
            dve.wait_ge(last_ready, 1)
            link(gated_sum(T - 1, 1, E - 2, acc[:, 1], acc[:, 1]))
            dve.wait_ge(last_ready, 2)
            gated_sum(T - 1, 1, E - 1, acc[:, 1], out_sb[:, T - 1]).then_inc(last_summed, 1)

        @block.tensor
        def _(pe):
            def transpose_weights(dst, w):
                for c in range(C):
                    for k in range(C):
                        last = nc.tensor.transpose(dst[:, c * H + k * P:c * H + (k + 1) * P],
                                                   w[:, k, c * P:(c + 1) * P], ident[:])
                return last

            def keep_warm(n):
                for _ in range(n):
                    nc.tensor.matmul(ring[BANKS - 1][:], warm[:, 0:P], warm[:], start=True, stop=True)

            pe.wait_ge(warm_ready, 1)
            pe.wait_ge(const_ready, 1)
            pe.wait_ge(wk_in, 16)
            transpose_weights(bank[0], wk_sb).then_inc(wkT_raw, 1)
            keep_warm(WARM[3])
            pe.wait_ge(key_in, 16 * 2)
            nc.tensor.transpose(bank[2][:, 0:2 * C], key_rows[:], ident[0:2 * C, 0:2 * C]).then_inc(key_vec_raw, 1)
            pe.wait_ge(kq_ready, 1)

            def key_query(c):
                for k in range(C):
                    last = nc.tensor.matmul(bank[2][:, c:c + 1], wk_sb[:, k, c * P:(c + 1) * P], kq[:, k:k + 1],
                                            start=(k == 0), stop=(k == C - 1))
                return last

            key_query(0)
            pe.wait_ge(x_sum_ready, 1)
            for c in range(C):
                last = nc.tensor.matmul(bank[4][:, c * NB:(c + 1) * NB], x_sum[:, c * P:(c + 1) * P], blk_sel[:],
                                        start=True, stop=True)
            last.then_inc(blk_raw, 1)
            key_query(1).then_inc(u_raw, 1)
            pe.wait_ge(blk_ready, 1)
            pe.wait_ge(wkT_ready, 1)
            for k in range(C):
                for c in range(C):
                    last = nc.tensor.matmul(bank[5][:, k * NB:(k + 1) * NB], wkT[:, c, k * P:(k + 1) * P], blkT[:, c],
                                            start=(c == 0), stop=(c == C - 1))
            last.then_inc(keys_ready, 1)
            pe.wait_ge(affine_in, 16 * 2)
            nc.tensor.transpose(bank[7][:, 0:2 * C], affine_rows[:],
                                ident[0:2 * C, 0:2 * C]).then_inc(affine_raw, 1)
            keep_warm(WARM[4])
            pe.wait_ge(ub_ready, 1)
            pe.wait_ge(key_sq_ready, 1)
            for c in range(C):
                last = nc.tensor.matmul(bank[6][:, 0:2 * NB], ones[:], to_sum[:, c].rearrange("p a n -> p (a n)"),
                                        start=(c == 0), stop=(c == C - 1))
            last.then_inc(key_sums_ready, 1)
            pe.wait_ge(wo_in, 16)
            transpose_weights(bank[1], wo_sb).then_inc(woT_raw, 1)
            keep_warm(WARM[0])
            pe.wait_ge(woT_ready, 1)
            pe.wait_ge(att_ready, 1)
            for c in range(C):
                last = nc.tensor.matmul(ps_proj[:, 0:H], att_bc[:, c], woT[:, c], start=(c == 0), stop=(c == C - 1))
            last.then_inc(proj_ready, 1)

            def transpose_tile(u, s):
                pe.wait_ge(z_ready, u + 1)
                for c in range(C):
                    dst = bank[5][:, 0:P] if c and isinstance(u, int) and u == 0 else ps_zT[:, c * P:(c + 1) * P]
                    last = nc.tensor.transpose(dst, z[:, s, c * P:(c + 1) * P], ident[:])
                last.then_inc(zT_ready, 1)

            TERMS = 3 * C
            ROUTES = 2 * C

            def route(u, s, k):
                c, h = k % C, (h_hi, h_lo)[k // C]
                if k == 0:
                    pe.wait_ge(hi_ready, u + 1)
                    if not isinstance(u, int) or u >= 1:
                        pe.wait_ge(gatesT_ready, u)
                if k == C:
                    pe.wait_ge(lo_ready, u + 1)
                ins = nc.tensor.matmul(ps_small[:, LOGITS], h[:, s, c], wr_2[:, c].rearrange("p a e -> p (a e)"),
                                       start=(k == 0), stop=(k == ROUTES - 1))
                if k == ROUTES - 1:
                    ins.then_inc(logits_ready, 1)

            def transpose_gates(t, s):
                pe.wait_ge(parts_ready, t + 1)
                nc.tensor.transpose(ps_small[0:3 * Q, GATES_T], gates_3[:, s], ident[:]).then_inc(gatesT_raw, 1)

            def bias(t, s):
                pe.wait_ge(gatesT_ready, t + 1)
                if not isinstance(t, int) or t >= 1:
                    pe.wait_ge(bias_staged, t)
                else:
                    pe.wait_ge(be_ready, 1)
                nc.tensor.matmul(ps_bias[:, 0:F], gatesT[:, s], be_3[:], start=True, stop=True).then_inc(bias_ready, 1)

            def terms_of(first=False):
                terms = [(h, w, c) for c in range(C) for h, w in ((h_hi, we_hi), (h_hi, we_lo), (h_lo, we_hi))]
                return sorted(terms, key=lambda term: term[0] is h_lo) if first else terms

            def experts(t, s, n, between=()):
                if not isinstance(t, int) or t >= 1:
                    pe.wait_ge(bank_free[n], t)
                else:
                    es = range(EB * (n + 1))
                    pe.wait_ge(we_lo_ready, sum(e not in LO_DVE for e in es))
                    pe.wait_ge(we_lo_dve, sum(e in LO_DVE for e in es))
                for k, (h, w, c) in enumerate(terms_of(isinstance(t, int) and t == 0 and n == 0)):
                    ins = nc.tensor.matmul(ring[n][:], h[:, s, c], w[:, EB * n:EB * (n + 1), c],
                                           start=(k == 0), stop=(k == TERMS - 1))
                    if k == TERMS - 1:
                        ins.then_inc(bank_ready[n], 1)
                    for at, issue in between:
                        if at == k:
                            issue()

            def routing(u, s, k0):
                return [(k0 + k, lambda k=k: route(u, s, k)) for k in range(ROUTES)]

            def last_experts(t, s):
                pe.wait_ge(bank_free[BANKS - 1], t)
                pe.wait_ge(bank_free[0], t + 1)
                for e in (E - 2, E - 1):
                    ps, at = expert_ps(t, e)
                    for k, (h, w, c) in enumerate(terms_of()):
                        ins = nc.tensor.matmul(ps[:, at:at + F], h[:, s, c], w[:, e, c],
                                               start=(k == 0), stop=(k == TERMS - 1))
                    ins.then_inc(last_ready, 1)

            def step(t, s, last):
                first = isinstance(t, int) and t == 0
                next_tile = (2, lambda: transpose_tile(t + 1, 1 - s))
                turn_gates = (TERMS - 1, lambda: transpose_gates(t, s))
                if first:
                    for k in range(C):
                        route(0, 0, k)
                    low_routes = [(2 * C - 1, lambda k=k: route(0, 0, k)) for k in range(C, ROUTES)]
                    experts(0, 0, 0, low_routes + [(TERMS - 1, lambda: transpose_tile(1, 1))])
                    experts(0, 0, 1)
                    experts(0, 0, 2, [turn_gates])
                    experts(0, 0, 3, routing(1, 1, 1) + [(TERMS - 1, lambda: bias(0, 0))])
                elif last:
                    experts(t, s, 0)
                    experts(t, s, 1, [turn_gates])
                    experts(t, s, 2, [(3, lambda: bias(t, s))])
                    last_experts(t, s)
                else:
                    experts(t, s, 0, [next_tile])
                    experts(t, s, 1, [turn_gates])
                    experts(t, s, 2, routing(t + 1, 1 - s, TERMS - ROUTES))
                    experts(t, s, 3, [(1, lambda: bias(t, s))])

            keep_warm(WARM[1])
            transpose_tile(0, 0)
            pe.wait_ge(wr_ready, 1)
            keep_warm(WARM[2])
            step(0, 0, False)
            step(1, 1, False)
            with pe.Fori(1, PAIRS - 1) as i:
                step(2 * i, 0, False)
                step(2 * i + 1, 1, False)
            step(T - 2, 0, False)
            step(T - 1, 1, True)


_INS = ['x', 'cond_2048', 'L0_cond_rms_weight', 'L0_cond_Wk', 'L0_cond_Wo', 'L0_cond_ln_gamma', 'L0_cond_ln_beta',
        'L0_ffn_Wr', 'L0_ffn_We', 'L0_ffn_be']
_OUTS = [((4, 256, 256), 'float32')]


def kernel(**inputs):
    import numpy as _np
    import concourse.bacc as _bacc
    from concourse import mybir as _mybir
    from concourse.bass_utils import run_bass_kernel_spmd as _run

    nc = _bacc.Bacc("TRN2", target_bir_lowering=False, num_devices=1)
    arrays, args = {}, []
    for name in _INS:
        a = _np.ascontiguousarray(inputs[name])
        arrays[f"in_{name}_dram"] = a
        args.append(nc.dram_tensor(f"in_{name}_dram", a.shape, _mybir.dt.from_np(a.dtype), kind="ExternalInput").ap())
    for i, (shape, dtype) in enumerate(_OUTS):
        dt = _mybir.dt.from_np(_np.dtype(dtype))
        args.append(nc.dram_tensor(f"out_{i}_dram", shape, dt, kind="ExternalOutput").ap())
    adaln_ffn_kernel(nc, *args)
    r = _run(nc, [arrays], core_ids=[0])
    got = tuple(r.results[0][f"out_{i}_dram"] for i in range(len(_OUTS)))
    return got[0]
```
